# Optimizing a Trainium2 kernel written in Bass

```python
import numpy as np
import jax
import jax.numpy as jnp

def _softmax(x, axis=-1):
    return jax.nn.softmax(x, axis=axis)

def _gelu(x):
    return jax.nn.gelu(x, approximate=True)

def _silu(x):
    return jax.nn.silu(x)

def _sigmoid(x):
    return jax.nn.sigmoid(x)

def _layernorm(x, axis=-1, eps=1e-05):
    m = jnp.mean(x, axis=axis, keepdims=True)
    v = jnp.var(x, axis=axis, keepdims=True)
    return (x - m) / jnp.sqrt(v + eps)

def _scatter_add(tgt, idx, src, axis=0):
    return tgt.at[idx].add(src)

def _segment_sum(src, seg, n):
    return jax.ops.segment_sum(src, seg, n)
kernel_name = 'mk_adaln_d1_jaxref_r8_98bcf5'

def setup_inputs(seed: int=0):
    np.random.seed(seed)
    _w = jnp.asarray

    def _L0_attn_setup():
        import jax, jax.numpy as jnp
        import numpy as np
        N_HEAD = 16
        LATENT = 32

        def _rotate_half(x):
            xe = x[..., ::2]
            xo = x[..., 1::2]
            return jnp.stack((-xo, xe), axis=-1).reshape(x.shape)

        def _rope_tables(T, latent_dim, dtype):
            inv_freq = 1.0 / 10000.0 ** (jnp.arange(0, latent_dim, 2, dtype=jnp.float32) / latent_dim)
            t = jnp.arange(T, dtype=jnp.float32)
            freqs = jnp.outer(t, inv_freq)
            cos = jnp.repeat(jnp.cos(freqs), 2, axis=-1)[:, :latent_dim]
            sin = jnp.repeat(jnp.sin(freqs), 2, axis=-1)[:, :latent_dim]
            return (cos.astype(dtype), sin.astype(dtype))
        key = jax.random.key(seed)
        ks = jax.random.split(key, 14)
        C = 128
        hd = C // N_HEAD
        L = LATENT
        s = 0.02
        return {'x': jax.random.normal(ks[0], (4, 256, C), jnp.float32), 'c_attn_w': jax.random.normal(ks[1], (3 * C, C), jnp.float32) * s, 'c_attn_b': jnp.zeros((3 * C,), jnp.float32), 'q2l_w': jax.random.normal(ks[2], (L, hd), jnp.float32) * s, 'q2l_b': jnp.zeros((L,), jnp.float32), 'kv2l_w': jax.random.normal(ks[3], (L, hd), jnp.float32) * s, 'kv2l_b': jnp.zeros((L,), jnp.float32), 'l2o_w': jax.random.normal(ks[4], (hd, L), jnp.float32) * s, 'l2o_b': jnp.zeros((hd,), jnp.float32), 'wqk_w': jax.random.normal(ks[5], (L, L), jnp.float32) * s, 'wqk_b': jnp.zeros((L,), jnp.float32), 'cproj_w': jax.random.normal(ks[6], (C, C), jnp.float32) * s, 'cproj_b': jnp.zeros((C,), jnp.float32)}
    _L0_attn_in = _L0_attn_setup()

    def _L0_ffn_setup():
        import jax, jax.numpy as jnp
        import numpy as np
        CAPACITY_FACTOR = 0.5
        key = jax.random.key(seed)
        ks = jax.random.split(key, 5)
        B, S, D, F = (4, 512, 128, 512)
        scale_in = 1.0 / np.sqrt(D)
        scale_ff = 1.0 / np.sqrt(F)
        return {'hidden_states': jax.random.normal(ks[0], (B, S, D), dtype=jnp.float32), 'w_router': jax.random.normal(ks[1], (D,), dtype=jnp.float32) * scale_in, 'W1': jax.random.normal(ks[2], (D, F), dtype=jnp.float32) * scale_in, 'b1': jnp.zeros((F,), dtype=jnp.float32), 'W2': jax.random.normal(ks[3], (F, D), dtype=jnp.float32) * scale_ff, 'b2': jnp.zeros((D,), dtype=jnp.float32)}
    _L0_ffn_in = _L0_ffn_setup()
    _L0_c = _w((lambda *s: np.random.randn(*s).astype(np.float32) * 0.05)(2, 128))
    _L0_wmod = _w((lambda *s: np.random.randn(*s).astype(np.float32) * 0.05)(128, 6 * 128) * 128 ** (-0.5))
    _d = {'L0_attn_x': _L0_attn_in['x'], 'L0_attn_c_attn_w': _L0_attn_in['c_attn_w'], 'L0_attn_c_attn_b': _L0_attn_in['c_attn_b'], 'L0_attn_q2l_w': _L0_attn_in['q2l_w'], 'L0_attn_q2l_b': _L0_attn_in['q2l_b'], 'L0_attn_kv2l_w': _L0_attn_in['kv2l_w'], 'L0_attn_kv2l_b': _L0_attn_in['kv2l_b'], 'L0_attn_l2o_w': _L0_attn_in['l2o_w'], 'L0_attn_l2o_b': _L0_attn_in['l2o_b'], 'L0_attn_wqk_w': _L0_attn_in['wqk_w'], 'L0_attn_wqk_b': _L0_attn_in['wqk_b'], 'L0_attn_cproj_w': _L0_attn_in['cproj_w'], 'L0_attn_cproj_b': _L0_attn_in['cproj_b'], 'L0_ffn_w_router': _L0_ffn_in['w_router'], 'L0_ffn_W1': _L0_ffn_in['W1'], 'L0_ffn_b1': _L0_ffn_in['b1'], 'L0_ffn_W2': _L0_ffn_in['W2'], 'L0_ffn_b2': _L0_ffn_in['b2'], 'L0_c': _L0_c, 'L0_wmod': _L0_wmod}
    _x0 = _d['L0_attn_x']
    _d['L0_attn_x'] = jax.random.normal(jax.random.fold_in(jax.random.key(seed), 1), (2, 1024, 128), dtype=_x0.dtype)
    del _x0
    return _d

def reference(L0_attn_x, L0_attn_c_attn_w, L0_attn_c_attn_b, L0_attn_q2l_w, L0_attn_q2l_b, L0_attn_kv2l_w, L0_attn_kv2l_b, L0_attn_l2o_w, L0_attn_l2o_b, L0_attn_wqk_w, L0_attn_wqk_b, L0_attn_cproj_w, L0_attn_cproj_b, L0_ffn_w_router, L0_ffn_W1, L0_ffn_b1, L0_ffn_W2, L0_ffn_b2, L0_c, L0_wmod):

    def _L0_attn_ref(x, c_attn_w, c_attn_b, q2l_w, q2l_b, kv2l_w, kv2l_b, l2o_w, l2o_b, wqk_w, wqk_b, cproj_w, cproj_b):
        import jax, jax.numpy as jnp
        import numpy as np
        N_HEAD = 16
        LATENT = 32

        def _rotate_half(x):
            xe = x[..., ::2]
            xo = x[..., 1::2]
            return jnp.stack((-xo, xe), axis=-1).reshape(x.shape)

        def _rope_tables(T, latent_dim, dtype):
            inv_freq = 1.0 / 10000.0 ** (jnp.arange(0, latent_dim, 2, dtype=jnp.float32) / latent_dim)
            t = jnp.arange(T, dtype=jnp.float32)
            freqs = jnp.outer(t, inv_freq)
            cos = jnp.repeat(jnp.cos(freqs), 2, axis=-1)[:, :latent_dim]
            sin = jnp.repeat(jnp.sin(freqs), 2, axis=-1)[:, :latent_dim]
            return (cos.astype(dtype), sin.astype(dtype))
        B, T, C = x.shape
        H = N_HEAD
        hd = C // H
        L = q2l_w.shape[0]
        qkv = x @ c_attn_w.T + c_attn_b
        q, k, v = jnp.split(qkv, 3, axis=2)

        def heads(t):
            return t.reshape(B, T, H, hd).transpose(0, 2, 1, 3)
        q, k, v = (heads(q), heads(k), heads(v))
        q_lat = q @ q2l_w.T + q2l_b
        k_lat = k @ kv2l_w.T + kv2l_b
        v_lat = v @ kv2l_w.T + kv2l_b
        cos, sin = _rope_tables(T, L, x.dtype)
        cos = cos[None, None]
        sin = sin[None, None]
        q_lat = q_lat * cos + _rotate_half(q_lat) * sin
        k_lat = k_lat * cos + _rotate_half(k_lat) * sin
        q_for_k = q_lat @ wqk_w.T + wqk_b
        att = jnp.einsum('bhql,bhkl->bhqk', q_for_k, k_lat) * L ** (-0.5)
        causal = jnp.tril(jnp.ones((T, T), dtype=bool))
        att = jnp.where(causal[None, None], att, -jnp.inf)
        att = jax.nn.softmax(att, axis=-1)
        y_lat = jnp.einsum('bhqk,bhkl->bhql', att, v_lat)
        y = y_lat @ l2o_w.T + l2o_b
        y = y.transpose(0, 2, 1, 3).reshape(B, T, C)
        return y @ cproj_w.T + cproj_b

    def _L0_ffn_ref(hidden_states, w_router, W1, b1, W2, b2):
        import jax, jax.numpy as jnp
        import numpy as np
        CAPACITY_FACTOR = 0.5
        'Mixture-of-Depths block: route top-k tokens through an FFN inner block,\n            scatter back with sigmoid router weights; bypassed tokens pass through.'
        B, S, D = hidden_states.shape
        k = int(S * CAPACITY_FACTOR)
        scores = jnp.einsum('bsd,d->bs', hidden_states, w_router)
        top_scores, top_idx = jax.lax.top_k(scores, k)
        weights = jax.nn.sigmoid(top_scores)
        selected = jnp.take_along_axis(hidden_states, top_idx[:, :, None], axis=1)
        h = jax.nn.gelu(jnp.einsum('bkd,df->bkf', selected, W1) + b1)
        processed = jnp.einsum('bkf,fd->bkd', h, W2) + b2
        update = weights[:, :, None] * processed

        def scatter_one(xb, ib, ub):
            return xb.at[ib].add(ub)
        output = jax.vmap(scatter_one)(hidden_states, top_idx, update)
        return output
    x = L0_attn_x
    mod = (_silu(L0_c) @ L0_wmod).reshape(L0_c.shape[0], 6, 1, -1)
    sa, ca, ga, sb, cb, gb = (mod[:, 0], mod[:, 1], mod[:, 2], mod[:, 3], mod[:, 4], mod[:, 5])
    ga = (2 * (ga >= 0) - 1) * jnp.maximum(jnp.abs(ga), 0.25)
    gb = (2 * (gb >= 0) - 1) * jnp.maximum(jnp.abs(gb), 0.25)
    h = _layernorm(x, axis=-1) * (1 + ca) + sa
    x = x + ga * _L0_attn_ref(h, L0_attn_c_attn_w, L0_attn_c_attn_b, L0_attn_q2l_w, L0_attn_q2l_b, L0_attn_kv2l_w, L0_attn_kv2l_b, L0_attn_l2o_w, L0_attn_l2o_b, L0_attn_wqk_w, L0_attn_wqk_b, L0_attn_cproj_w, L0_attn_cproj_b)
    h = _layernorm(x, axis=-1) * (1 + cb) + sb
    x = x + gb * _L0_ffn_ref(h, L0_ffn_w_router, L0_ffn_W1, L0_ffn_b1, L0_ffn_W2, L0_ffn_b2)
    return x

_drawn_inputs = setup_inputs


def setup_inputs(seed=0):
    import zlib

    import numpy as np

    out = dict(_drawn_inputs(seed))
    spreads = {'L0_attn_c_attn_b': (0.0, 0.8),
     'L0_attn_q2l_b': (0.0, 0.8),
     'L0_attn_kv2l_b': (0.0, 0.8),
     'L0_attn_l2o_b': (0.0, 0.8),
     'L0_attn_wqk_b': (0.0, 0.8),
     'L0_attn_cproj_b': (0.0, 0.328),
     'L0_ffn_b1': (0.0, 0.8),
     'L0_ffn_b2': (0.0, 0.661)}
    factors = {'L0_attn_c_attn_w': 8.0,
     'L0_attn_q2l_w': 8.0,
     'L0_attn_kv2l_w': 8.0,
     'L0_attn_l2o_w': 8.0,
     'L0_attn_wqk_w': 8.0,
     'L0_attn_cproj_w': 8.0}
    for name, (base, spread) in spreads.items():
        noise = np.random.default_rng([zlib.crc32(name.encode()), seed]).standard_normal(out[name].shape)
        drawn = base * np.exp(spread * noise) if base else spread * noise
        out[name] = jnp.asarray(drawn.astype(out[name].dtype))
    for name, factor in factors.items():
        out[name] = (out[name] * factor).astype(out[name].dtype)
    return out
```

```python
from contextlib import ExitStack

import numpy as np
import concourse.bass as bass
from concourse import mybir

F32 = mybir.dt.float32
F32R = mybir.dt.float32r
BF16 = mybir.dt.bfloat16
ACT = mybir.ActivationFunctionType
ALU = mybir.AluOpType
AX = mybir.AxisListType

B, T, C = 2, 1024, 128
H, HD, L = 16, 8, 32
F = 512
KEEP = T // 2
G = 4
NG = H // G
NU = B * NG
NT = T // 128
QD = B * T // 512
FT = F // 128
SR = 3 * L
CR = SR + 2
NEG = -3.0e38
MASKED = -1.0e30
EPS = 1e-5

CHUNKS = [(q, k, max(0, 128 * k - 512 * q), 512 - max(0, 128 * k - 512 * q))
          for q in range(2) for k in range(4 * (q + 1))]
NC = len(CHUNKS)
DIAG = [n for n, (q, k, _, _) in enumerate(CHUNKS) if 128 * k >= 512 * q]
LAST = [3, NC - 1]
MAXES = [(j, i, part) for j in range(G) for i in range(NT) for part in range(1 + (i >= 4))]
NM = len(MAXES)
RING = 3
LAG = 2


def spread(n):
    steps = list(range(1, NC - 1))
    total, out, done, at = sum(CHUNKS[s][3] for s in steps), [[] for _ in range(NC)], 0, 0
    for s in steps:
        at += CHUNKS[s][3]
        upto = round(n * at / total)
        out[s] = list(range(done, upto))
        done = upto
    return out


MAX_STEPS = spread(NM)
PROJ = [(0, 0, 0), (0, 0, 1), (0, 1, 0), (0, 1, 1), (1, 0, 0), (1, 0, 1), (1, 1, 0), (1, 1, 1)]
PROJ_STEP = [0, 1, 2, 3, 5, 6, 7, 8]
WQK_STEP = [4, 6]
ROPE_STEP = {2: (0, 0), 4: (0, 1), 7: (1, 0), 9: (1, 1)}
KH_STEP = [8, 10]
KL_STEP = [9, 11]


def adaln_block(nc, d, out):
    with ExitStack() as ctx:
        def sb(name, shape, dt=F32):
            return ctx.enter_context(nc.sbuf_tensor(name, shape, dt))

        def sem(name):
            return ctx.enter_context(nc.semaphore(name))

        xs = sb("xs", [128, B * NT, C])
        ident = sb("ident", [128, 128])
        identb = sb("identb", [128, 128], BF16)
        maskb = sb("maskb", [128, 128], BF16)
        ones = sb("ones", [128, 128])
        cosT = sb("cosT", [128, T])
        sinT = sb("sinT", [128, T])
        cT = sb("cT", [128, B])
        cols = sb("cols", [128, 16])
        wsplit = sb("wsplit", [SR, 4, 128], F32R)
        wqk = sb("wqk", [128, 128])
        bqk = sb("bqk", [128, 1])
        cpT = sb("cpT", [128, C])
        l2oT = sb("l2oT", [L, 128])
        kvrep = sb("kvrep", [L, 128])
        kvb = sb("kvb", [L, 1])
        blockd = sb("blockd", [128, 128])
        tri = sb("tri", [128, 128])
        wrb = sb("wrb", [128, 128])
        bvb = sb("bvb", [128, C])
        w1 = sb("w1", [128, F])
        w2g = sb("w2g", [128, B, FT, C])
        woT = sb("woT", [128, B, C])
        bc = sb("bc", [128, 6, B, C])
        modc = sb("modc", [128, 6, B])
        gate = sb("gate", [128, 10, B])
        m8 = sb("m8", [128, 128])
        yb = sb("yb", [128, 4])
        vnat = sb("vnat", [128, B * NT, C])
        vu = [sb(f"vu{p}", [128, NT, G, 32]) for p in range(2)]
        parts = sb("parts", [128, 4, T], F32R)
        rope = sb("rope", [128, 2, T])
        s8 = sb("s8", [SR, 2, T], F32R)
        probs = sb("probs", [128, RING, G, 512])
        oT = sb("oT", [128, NU, T])
        pm = [sb(f"pm{p}", [128, G, NT, 2]) for p in range(2)]
        nm = sb("nm", [128, G * NT])
        nms = sb("nms", [128, 2, G * NT], F32R)
        nmT = sb("nmT", [2 * G * NT, 128])
        bst = sb("bst", [128, B * NT, 6])
        mv = sb("mv", [128, B * NT, 2])
        std = sb("std", [128, B * NT])
        rstd = sb("rstd", [128, B * NT])
        epsc = sb("epsc", [128, 1])
        onesb = sb("onesb", [128, 2], BF16)
        scol = sb("scol", [128, B * NT])
        wsel = sb("wsel", [128, B * NT])
        sig = sb("sig", [128, B * NT])

        with ExitStack() as shared:
            stack = [shared.enter_context(nc.sbuf_tensor(f"stack{p}", [128, 2, G, T], F32R))
                     for p in range(2)]
        late, late2 = sb("late", [128, 2 * G * T]), sb("late2", [128, 2 * G * T])

        early = oT[:].rearrange("p u t -> p (u t)")
        hT = early[:, 0:2048]
        zn = early[:, 2048:4096].rearrange("p (t c) -> p t c", c=C)
        wmod = early[:, 4096:4864]
        wqkvT = early[:, 4864:5248]
        diag = early[:, 5248:6784].rearrange("p (r b c) -> p r b c", r=6, b=B)
        wraw = early[0:SR, 6784:7296].rearrange("p (k m) -> p k m", k=4)
        whi = parts[0:SR, 0, 0:512].rearrange("p (k m) -> p k m", k=4)
        q8 = stack[1][:].rearrange("p a j t -> p (a j t)").rearrange("p (k n) -> p k n", k=4)
        ynat = late[:, 0:1024].rearrange("p (s t c) -> p s t c", s=2, c=C)
        yT = late[:, 1024:2048].rearrange("p (s n) -> p s n", s=2)
        z2 = late[:, 2048:4096].rearrange("p (t c) -> p t c", c=C)
        h2T = late[:, 4096:6144]
        srow = late[:, 6144:8192]
        actT = late2[:, 0:4096].rearrange("p (s f n) -> p s f n", s=2, f=FT)
        res = late2[:, 4096:6144].rearrange("p (t c) -> p t c", c=C)
        proc = late2[:, 6144:8192].rearrange("p (t c) -> p t c", c=C)
        lateP = probs[:].rearrange("p r j n -> p (r j n)")
        smask = lateP[:, 0:1024]
        fin = lateP[:, 1024:3072].rearrange("p (t c) -> p t c", c=C)
        eqm = lateP[:, 3072:4096]
        recd = lateP[:, 4096:4224].rearrange("p (s n) -> p s n", s=2)
        before = [rope[:, n // 2, :].bitcast(BF16)[:, T * (n % 2):T * (n % 2) + T] for n in range(4)] + \
                 [t[:].bitcast(BF16)[:, T * n:T * n + T] for t in (cosT, sinT) for n in range(2)]

        ps = ctx.enter_context(nc.psum_tensor("ps", [128, 8, 512], F32))
        E = [ps[:, 0:2, :], ps[:, 2:4, :]]
        M = [ps[:, 4, :], ps[:, 5, :]]
        O = ps[:, 6, :]
        X = ps[:, 7, :]

        x_in = [sem(f"x_in{i}") for i in range(QD)]
        mod_in, qkv_in, attn_in, ffn_in, const_in = (sem(n) for n in (
            "mod_in", "qkv_in", "attn_in", "ffn_in", "const_in"))
        memsets = sem("memsets")
        silu_e, silu_done, mod_mm, mod_done = (sem(n) for n in ("silu_e", "silu_done", "mod_mm", "mod_done"))
        gates_done, diag_done, bc_mm, bc_done = (sem(n) for n in ("gates_done", "diag_done", "bc_mm", "bc_done"))
        m8_mm, m8_done, yb_mm, yb_done, wo_mm, wo_done = (sem(n) for n in (
            "m8_mm", "m8_done", "yb_mm", "yb_done", "wo_mm", "wo_done"))
        dve_step = sem("dve_step")
        stats, std_done, zn_done, zn_tr, hT_done = (sem(n) for n in (
            "stats", "std_done", "zn_done", "zn_tr", "hT_done"))
        qk_mm, qkH_done, qkL_done, v_mm, v_done = (sem(n) for n in (
            "qk_mm", "qkH_done", "qkL_done", "v_mm", "v_done"))
        wsplit_done, xadd_done, w2g_done = (sem(n) for n in ("wsplit_done", "xadd_done", "w2g_done"))
        q8_out, s8_in = [sem(f"q8_out{b}") for b in range(B)], sem("s8_in")
        proj_mm, proj_ev, rope_done, rope_step = (sem(n) for n in ("proj_mm", "proj_ev", "rope_done", "rope_step"))
        wqk_mm, qH_done, qL_done, kH_done, kL_done = (sem(n) for n in (
            "wqk_mm", "qH_done", "qL_done", "kH_done", "kL_done"))
        head_in = [sem(f"head_in{j}") for j in range(G)]
        row_in, vu_done = sem("row_in"), sem("vu_done")
        max_mm, max_done, nm_step, nm_done, nm_tr, nmT_done = (sem(n) for n in (
            "max_mm", "max_done", "nm_step", "nm_done", "nm_tr", "nmT_done"))
        score_mm, exp_done, sel_done, pv_mm, o_done = (sem(n) for n in (
            "score_mm", "exp_done", "sel_done", "pv_mm", "o_done"))
        tr1, rec_done, ynat_done, tr2, yT_done, x1_mm, x1_done = (sem(n) for n in (
            "tr1", "rec_done", "ynat_done", "tr2", "yT_done", "x1_mm", "x1_done"))
        stats2, std2, z2_done, tr3, h2T_done, sc_mm, srow_done = (sem(n) for n in (
            "stats2", "std2", "z2_done", "tr3", "h2T_done", "sc_mm", "srow_done"))
        f1_mm, gelu_done, f2_mm, proc_done, res_step, res_done = (sem(n) for n in (
            "f1_mm", "gelu_done", "f2_mm", "proc_done", "res_step", "res_done"))
        scol_done, gt_done, rank_mm, sig_done, fin_done, out_done = (sem(n) for n in (
            "scol_done", "gt_done", "rank_mm", "sig_done", "fin_done", "out_done"))

        scratch = nc.dram_tensor("q8_scratch", [128, 4, B * T], F32, kind="Internal").ap()

        block = ctx.enter_context(nc.Block())

        CA, SA, CB, SBC, GA, GAO, GB, GBC, GBS, GB2 = range(10)
        ROWS = [GA, GAO, GB, GBC, GBS, GB2]
        BQ, BK, QB, QRB, KB, KRB, WB, LOB, CPB, B2 = range(10)
        B1 = 10

        @block.sync
        def _(sp):
            xd = d["x"].rearrange("b (t p) c -> p (b t) c", p=128)
            for i in range(QD):
                sp.dma_start(xs[:, 4 * i:4 * i + 4, :], xd[:, 4 * i:4 * i + 4, :]).then_inc(x_in[i], 16)
                if i == 0:
                    sp.dma_start(ident[:], d["ident"]).then_inc(const_in, 16)
            sp.dma_start(cosT[:], d["cos"]).then_inc(attn_in, 16)
            sp.dma_start(sinT[:], d["sin"]).then_inc(attn_in, 16)
            for dst, name in ((w1[:], "w1"), (w2g[:, 0], "w2"), (w2g[:, 1], "w2"), (wrb[:], "wr")):
                sp.dma_start(dst, d[name]).then_inc(ffn_in, 16)
            for b in range(B):
                sp.wait_ge(qkH_done, 4 * (b + 1))
                sp.wait_ge(qkL_done, 4 * (b + 1))
                sp.dma_start(scratch[:, :, b * T:(b + 1) * T],
                             q8[:, :, b * T:(b + 1) * T].bitcast(F32)).then_inc(q8_out[b], 16)

            def load_s8(u):
                b, g = (u // NG, u % NG)
                for s, part in enumerate((0, 1, 0)):
                    src = scratch[g * 32:(g + 1) * 32, part::2, b * T:(b + 1) * T]
                    sp.dma_start(s8[s * 32:(s + 1) * 32, :, :].bitcast(F32), src).then_inc(s8_in, 16)

            for t in range(-2, NU):
                par = t % 2
                if t == -2:
                    sp.wait_ge(q8_out[0], 16)
                    load_s8(0)
                if 0 <= t + 1 < NU:
                    v = t + 1
                    sp.wait_ge(qH_done, 2 * (v + 1))
                    sp.wait_ge(qL_done, 2 * (v + 1))
                    sp.wait_ge(kH_done, 2 * (v + 1))
                    sp.wait_ge(kL_done, 2 * (v + 1))
                    if t >= 1:
                        sp.wait_ge(pv_mm, NC * t)
                    if v == 1:
                        for b in range(B):
                            sp.wait_ge(q8_out[b], 16)
                    st = stack[1 - par]
                    for j in range(G):
                        for s, (a, c) in enumerate(((0, 2), (1, 2), (0, 3))):
                            sp.dma_start(st[s * 32:(s + 1) * 32, :, j, :].bitcast(F32),
                                         parts[j * 32:(j + 1) * 32, a:c + 1:c - a, :].bitcast(F32)
                                         ).then_inc(head_in[j], 16)
                if t + 3 < NU:
                    sp.wait_ge(proj_mm, 8 * (t + 3))
                    if t + 3 == NG:
                        sp.wait_ge(q8_out[1], 16)
                    load_s8(t + 3)
                if 0 <= t + 1 < NU:
                    sp.wait_ge(nmT_done, t + 2)
                    for hl in range(2):
                        row = stack[1 - par][SR + hl:SR + hl + 1, 0, :, :].bitcast(F32)
                        sp.dma_start(row.rearrange("o j (i n) -> o (j i) n", n=128),
                                     nmT[hl * 32:(hl + 1) * 32, :]).then_inc(row_in, 16)
            od = out.rearrange("b (t p) c -> p (b t) c", p=128)
            for i in range(QD):
                sp.wait_ge(fin_done, 4 * (i + 1))
                sp.dma_start(od[:, 4 * i:4 * i + 4, :], fin[:, 4 * i:4 * i + 4, :]).then_inc(out_done, 16)
            sp.wait_ge(out_done, 16 * QD)

        @block.scalar
        def _(act):
            for dst, name in ((cT[:], "cT"), (wmod, "wmod"), (cols[:], "cols")):
                act.dma_start(dst, d[name]).then_inc(mod_in, 16)
            for dst, name in ((wqkvT, "wqkvT"), (bvb[:], "bv"), (wraw, "wlat")):
                act.dma_start(dst, d[name]).then_inc(qkv_in, 16)
            for dst, name in ((wqk[:], "wqk"), (cpT[:], "cpT"), (l2oT[:], "l2oT"), (kvrep[:], "kvrep"),
                              (kvb[:], "kvb"), (blockd[:], "blockd"), (tri[:], "tri")):
                act.dma_start(dst, d[name]).then_inc(attn_in, 16)
            act.wait_ge(mod_in, 48)
            nc.scalar.activation(sig[:, 0:B], cT[:], ACT.Exp, scale=-1.0).then_inc(silu_e, 1)
            act.wait_ge(memsets, 1)
            for i in range(QD):
                act.wait_ge(stats, 4 * (i + 1))
                nc.scalar.activation(std[:, 4 * i:4 * i + 4], mv[:, 4 * i:4 * i + 4, 1], ACT.Sqrt,
                                     bias=epsc[:, 0:1]).then_inc(std_done, 1)

            def qk_high(i, a):
                act.wait_ge(qk_mm, 2 * i + a + 1)
                nc.scalar.activation(q8[:, 2 * a, 512 * i:512 * i + 512], ps[:, 2 + a, :], ACT.Identity,
                                     bias=cols[:, BQ + a:BQ + a + 1]).then_inc(qkH_done, 1)

            act.wait_ge(gates_done, 4)
            for i in range(QD):
                b = i // 2
                act.wait_ge(zn_tr, i + 1)
                nc.scalar.activation(hT[:, 512 * i:512 * i + 512], ps[:, i % 2, :], ACT.Identity,
                                     bias=gate[:, SA, b:b + 1], scale=gate[:, CA, b:b + 1]).then_inc(hT_done, 1)
                if i:
                    qk_high(i - 1, 0)
                    qk_high(i - 1, 1)
            qk_high(QD - 1, 0)
            qk_high(QD - 1, 1)
            for n in range(3):
                act.wait_ge(bc_mm, n + 1)
                nc.scalar.copy(bc[:].rearrange("p r b c -> p (r b c)")[:, 512 * n:512 * n + 512],
                               ps[:, 5 + n, :]).then_inc(bc_done, 1)

            def projected(t, n):
                a, half, rot = PROJ[n]
                u = t + 2
                act.wait_ge(proj_mm, 8 * u + n + 1)
                if a == 0 and u > 0:
                    act.wait_ge(kH_done, 2 * u - 1 + half)
                    act.wait_ge(kL_done, 2 * u - 1 + half)
                if a == 1:
                    act.wait_ge(wqk_mm, 2 * u + half + 1)
                bias = cols[:, QB + 2 * a + rot:QB + 2 * a + rot + 1]
                nc.scalar.activation(rope[:, rot, 512 * half:512 * half + 512], X, ACT.Identity,
                                     bias=bias).then_inc(proj_ev, 1)

            def q_high(t, half):
                u = t + 2
                act.wait_ge(wqk_mm, 2 * u + half + 1)
                for j in range(G):
                    if u >= 1:
                        act.wait_ge(head_in[j], 48 * u)
                nc.scalar.activation(parts[:, 0, 512 * half:512 * half + 512], X, ACT.Identity,
                                     bias=bqk[:, 0:1]).then_inc(qH_done, 1)

            def k_high(t, half):
                u = t + 2
                act.wait_ge(rope_done, 4 * u + 2 + half + 1)
                if u >= 1:
                    for j in range(G):
                        act.wait_ge(head_in[j], 48 * u)
                nc.scalar.copy(parts[:, 2, 512 * half:512 * half + 512],
                               rope[:, 0, 512 * half:512 * half + 512]).then_inc(kH_done, 1)

            def exps(t, c, pair):
                q, k, off, w = CHUNKS[c]
                act.wait_ge(score_mm, 2 * NC * t + 2 * c + pair + 1)
                if NC * t + c >= RING:
                    act.wait_ge(pv_mm, NC * t + c - RING + 1)
                nc.scalar.activation(probs[:, c % RING, 2 * pair:2 * pair + 2, 0:w], E[pair][:, :, 0:w],
                                     ACT.Exp).then_inc(exp_done, 1)

            def o_copy(t, q):
                act.wait_ge(pv_mm, NC * t + LAST[q] + 1)
                nc.scalar.copy(oT[:, t, 512 * q:512 * q + 512], O).then_inc(o_done, 1)

            act.wait_ge(attn_in, 144)
            for t in range(-2, NU):
                for c in range(NC):
                    if t >= 0:
                        exps(t, c, 0)
                        if c == LAST[0] + LAG + 1:
                            o_copy(t, 0)
                        exps(t, c, 1)
                    if t + 2 < NU:
                        if c in WQK_STEP:
                            q_high(t, WQK_STEP.index(c))
                        if c in PROJ_STEP:
                            projected(t, PROJ_STEP.index(c))
                        if c in KH_STEP:
                            k_high(t, KH_STEP.index(c))
                    if c == NC - 1 and 0 <= t + 1 < NU:
                        act.wait_ge(nm_tr, t + 2)
                        if t >= 0:
                            act.wait_ge(row_in, 32 * (t + 1))
                        nc.scalar.copy(nmT[:], ps[0:64, 7, 0:128]).then_inc(nmT_done, 1)
                if t >= 0:
                    o_copy(t, 1)

            def part_a(i):
                s = i % 2
                act.wait_ge(tr2, i + 1)
                if i >= 2:
                    act.wait_ge(x1_mm, i - 1)
                nc.scalar.copy(yT[:, s, :], ps[:, 4, :]).then_inc(yT_done, 1)
                act.wait_ge(stats2, 4 * (i + 1))
                nc.scalar.activation(std[:, 4 * i:4 * i + 4], mv[:, 4 * i:4 * i + 4, 1], ACT.Sqrt,
                                     bias=epsc[:, 0:1]).then_inc(std2, 1)

            def part_b(i):
                b, s = i // 2, i % 2
                act.wait_ge(tr3, i + 1)
                nc.scalar.activation(h2T[:, 512 * i:512 * i + 512], ps[:, 6, :], ACT.Identity,
                                     bias=gate[:, SBC, b:b + 1], scale=gate[:, CB, b:b + 1]).then_inc(h2T_done, 1)
                act.wait_ge(sc_mm, i + 1)
                nc.scalar.copy(srow[:, 512 * i:512 * i + 512], ps[:, 7, :]).then_inc(srow_done, 1)
                for f in range(FT):
                    act.wait_ge(f1_mm, FT * i + f + 1)
                    if i >= 2:
                        act.wait_ge(f2_mm, i - 1)
                    nc.scalar.activation(actT[:, s, f, :], ps[:, f, :], ACT.Gelu_apprx_tanh,
                                         bias=cols[:, B1 + f:B1 + f + 1]).then_inc(gelu_done, 1)

            def weights(b):
                act.wait_ge(scol_done, b + 1)
                nc.scalar.activation(sig[:, NT * b:NT * b + NT], scol[:, NT * b:NT * b + NT],
                                     ACT.Sigmoid).then_inc(sig_done, 1)

            part_a(0)
            part_a(1)
            part_b(0)
            part_a(2)
            part_b(1)
            weights(0)
            part_a(3)
            part_b(2)
            part_b(3)
            weights(1)

        @block.gpsimd
        def _(pool):
            pool.wait_ge(zn_done, QD)
            pool.wait_ge(bc_done, 3)
            for b in range(B):
                nc.gpsimd.tensor_tensor(xs[:, NT * b:NT * b + NT, :], xs[:, NT * b:NT * b + NT, :],
                                        bc[:, 1, b:b + 1, :].to_broadcast([128, NT, C]), ALU.add).then_inc(xadd_done, 1)
            pool.wait_ge(ffn_in, 64)
            for b in range(B):
                nc.gpsimd.tensor_tensor(w2g[:, b], w2g[:, b], bc[:, 2, b:b + 1, :].to_broadcast([128, FT, C]),
                                        ALU.mult).then_inc(w2g_done, 1)
            steps = [0]

            def rotate(t, a, half):
                u = t + 2
                n = 512 * half
                for rot, table in ((0, cosT), (1, sinT)):
                    pool.wait_ge(proj_ev, 8 * u + PROJ.index((a, half, rot)) + 1)
                    r = rope[:, rot, n:n + 512]
                    nc.gpsimd.tensor_tensor(r, r, table[:, n:n + 512], ALU.mult).then_inc(rope_step, 1)
                    steps[0] += 1
                pool.wait_ge(rope_step, steps[0])
                nc.gpsimd.tensor_tensor(rope[:, 0, n:n + 512], rope[:, 0, n:n + 512], rope[:, 1, n:n + 512],
                                        ALU.add).then_inc(rope_done, 1)

            def k_low(t, half):
                u = t + 2
                pool.wait_ge(kH_done, 2 * u + half + 1)
                n = slice(512 * half, 512 * half + 512)
                nc.gpsimd.tensor_tensor(parts[:, 3, n], rope[:, 0, n], parts[:, 2, n].bitcast(F32),
                                        ALU.subtract).then_inc(kL_done, 1)

            pool.wait_ge(attn_in, 144)
            for t in range(-2, NU):
                for c in range(NC):
                    if t >= 0 and c in DIAG:
                        pool.wait_ge(exp_done, 2 * NC * t + 2 * c + 2)
                        p = probs[:, c % RING, :, 0:128]
                        nc.gpsimd.affine_select(out=p, in_=p, compare_op=ALU.is_ge, fill=0.0, base=0,
                                                pattern=[[0, G], [1, 128]], channel_multiplier=-1).then_inc(sel_done, 1)
                    if t + 2 < NU:
                        if c in ROPE_STEP:
                            rotate(t, *ROPE_STEP[c])
                        if c in KL_STEP:
                            k_low(t, KL_STEP.index(c))

            for i in range(QD):
                b = i // 2
                q = slice(4 * i, 4 * i + 4)
                pool.wait_ge(z2_done, i + 1)
                nc.gpsimd.tensor_tensor(res[:, q, :], z2[:, q, :], bc[:, 3, b:b + 1, :].to_broadcast([128, 4, C]),
                                        ALU.mult).then_inc(res_step, 1)
                pool.wait_ge(res_step, 2 * i + 1)
                nc.gpsimd.tensor_tensor(res[:, q, :], res[:, q, :], xs[:, q, :], ALU.add).then_inc(res_step, 1)
                pool.wait_ge(res_step, 2 * i + 2)
                nc.gpsimd.tensor_tensor(res[:, q, :], res[:, q, :], bc[:, 4, b:b + 1, :].to_broadcast([128, 4, C]),
                                        ALU.add).then_inc(res_done, 1)

        @block.vector
        def _(dve):
            chain = [0]

            def then(ins):
                chain[0] += 1
                ins.then_inc(dve_step, 1)
                dve.wait_ge(dve_step, chain[0])

            nc.vector.memset(epsc[:], EPS).then_inc(memsets, 1)
            nc.vector.memset(ones[:], 1.0).then_inc(memsets, 1)
            nc.vector.memset(onesb[:], 1.0).then_inc(memsets, 1)
            for p in range(2):
                nc.vector.memset(pm[p][:], NEG).then_inc(memsets, 1)
                then(nc.vector.memset(vu[p][:], 0.0))
                nc.vector.memset(vu[p][:, :, :, HD:HD + 1], 1.0).then_inc(memsets, 1)
            nc.vector.memset(stack[0][SR:CR, 1, :, :].bitcast(F32), 1.0).then_inc(memsets, 1)

            def norm_stats(i, done):
                for n in range(4 * i, 4 * i + 4):
                    ins = nc.vector.bn_stats(bst[:, n, :], xs[:, n, :])
                then(ins)
                for n in range(4 * i, 4 * i + 4):
                    nc.vector.bn_aggr(mv[:, n, :], bst[:, n, :]).then_inc(done, 1)

            def normalise(i, dst, src_std, out_sem):
                dve.wait_ge(src_std, i + 1)
                then(nc.vector.reciprocal(rstd[:, 4 * i:4 * i + 4], std[:, 4 * i:4 * i + 4]))
                for n in range(4 * i, 4 * i + 4):
                    ins = nc.vector.tensor_scalar(dst[:, n, :], xs[:, n, :], mv[:, n, 0:1], rstd[:, n:n + 1],
                                                  ALU.subtract, ALU.mult)
                ins.then_inc(out_sem, 1)

            for i in range(QD):
                dve.wait_ge(x_in[i], 16)
                norm_stats(i, stats)
                if i == 1:
                    dve.wait_ge(silu_e, 1)
                    then(nc.vector.tensor_scalar(sig[:, 2:4], sig[:, 0:2], 1.0, None, ALU.add))
                    then(nc.vector.reciprocal(sig[:, 4:6], sig[:, 2:4]))
                    nc.vector.tensor_tensor(sig[:, 6:8], sig[:, 4:6], cT[:], ALU.mult).then_inc(silu_done, 1)
                if i >= 1:
                    normalise(i - 1, zn, std_done, zn_done)
            dve.wait_ge(qkv_in, 48)
            then(nc.vector.tensor_copy(whi, wraw))
            nc.vector.tensor_copy(wsplit[0:64], wraw[0:64]).then_inc(wsplit_done, 1)
            nc.vector.tensor_tensor(wsplit[64:SR], wraw[64:SR], whi[64:SR].bitcast(F32),
                                    ALU.subtract).then_inc(wsplit_done, 1)
            normalise(QD - 1, zn, std_done, zn_done)
            dve.wait_ge(mod_mm, 1)
            then(nc.vector.tensor_copy(modc[:].rearrange("p k b -> p (k b)"), ps[:, 6, 0:12]))
            nc.vector.tensor_scalar(gate[:, CA, :], modc[:, 1, :], 1.0, None, ALU.add).then_inc(gates_done, 1)
            nc.vector.tensor_copy(gate[:, SA, :], modc[:, 0, :]).then_inc(gates_done, 1)
            nc.vector.tensor_scalar(gate[:, CB, :], modc[:, 4, :], 1.0, None, ALU.add).then_inc(gates_done, 1)
            nc.vector.tensor_copy(gate[:, SBC, :], modc[:, 3, :]).then_inc(gates_done, 1)

            def qk_low(i, a):
                dve.wait_ge(qkH_done, 2 * i + a + 1)
                n = slice(512 * i, 512 * i + 512)
                nc.vector.scalar_tensor_tensor(out=q8[:, 2 * a + 1, n], in0=ps[:, 2 + a, :],
                                               scalar=cols[:, BQ + a:BQ + a + 1], in1=q8[:, 2 * a, n].bitcast(F32),
                                               op0=ALU.add, op1=ALU.subtract).then_inc(qkL_done, 1)

            def v_copy(i):
                dve.wait_ge(v_mm, i + 1)
                nc.vector.tensor_tensor(vnat[:, 4 * i:4 * i + 4, :], ps[:, 4, :].rearrange("p (t c) -> p t c", c=C),
                                        bvb[:].rearrange("p (o c) -> p o c", o=1).to_broadcast([128, 4, C]),
                                        ALU.add).then_inc(v_done, 1)

            for i in range(QD):
                qk_low(i, 0)
                qk_low(i, 1)
                v_copy(i)
            for src, dst in ((2, GA), (5, GB)):
                g = modc[:, src, :]
                then(nc.vector.tensor_scalar(sig[:, 8:10], g, 0.25, None, ALU.max))
                then(nc.vector.scalar_tensor_tensor(out=sig[:, 10:12], in0=g, scalar=-1.0, in1=sig[:, 8:10],
                                                    op0=ALU.mult, op1=ALU.max))
                then(nc.vector.tensor_scalar(sig[:, 12:14], g, 0.0, 2.0, ALU.is_ge, ALU.mult))
                then(nc.vector.scalar_tensor_tensor(out=gate[:, dst, :], in0=sig[:, 12:14], scalar=-1.0,
                                                    in1=sig[:, 10:12], op0=ALU.add, op1=ALU.mult))
            then(nc.vector.tensor_tensor(gate[:, GBC, :], gate[:, GB, :], gate[:, CB, :], ALU.mult))
            then(nc.vector.tensor_tensor(gate[:, GBS, :], gate[:, GB, :], gate[:, SBC, :], ALU.mult))
            then(nc.vector.tensor_scalar(gate[:, GB2, :], gate[:, GB, :], cols[:, B2:B2 + 1], None, ALU.mult))
            dve.wait_ge(m8_mm, 1)
            nc.vector.tensor_tensor(m8[:], ps[:, 5, 0:128], blockd[:], ALU.mult).then_inc(m8_done, 1)
            dve.wait_ge(yb_mm, 1)
            nc.vector.tensor_tensor(yb[:, 0:1], ps[:, 6, 128:129], cols[:, LOB:LOB + 1], ALU.add).then_inc(yb_done, 1)
            dve.wait_ge(yb_mm, 2)
            then(nc.vector.tensor_tensor(yb[:, 1:2], ps[:, 6, 256:257], cols[:, CPB:CPB + 1], ALU.add))
            then(nc.vector.tensor_scalar(gate[:, GAO, :], gate[:, GA, :], yb[:, 1:2], None, ALU.mult))
            dve.wait_ge(const_in, 16)
            for r, which in enumerate(ROWS):
                for b in range(B):
                    ins = nc.vector.tensor_scalar(diag[:, r, b, :], ident[:], gate[:, which, b:b + 1], None, ALU.mult)
            ins.then_inc(diag_done, 1)
            dve.wait_ge(wo_mm, 1)
            dve.wait_ge(bc_done, 3)
            for b in range(B):
                ins = nc.vector.tensor_tensor(woT[:, b, :], ps[:, 4, 0:128], bc[:, 0, b, :], ALU.mult)
            ins.then_inc(wo_done, 1)
            dve.wait_ge(attn_in, 144)
            nc.vector.tensor_copy(identb[:], ident[:]).then_inc(memsets, 1)
            nc.vector.tensor_scalar(maskb[:], tri[:], MASKED, None, ALU.mult).then_inc(memsets, 1)
            then(nc.vector.tensor_scalar(wqk[:], wqk[:], float(L) ** -0.5, None, ALU.mult))
            nc.vector.tensor_scalar(bqk[:], cols[:, WB:WB + 1], float(L) ** -0.5, None, ALU.mult).then_inc(wo_done, 1)
            for b in range(B):
                dve.wait_ge(q8_out[b], 16)
            nc.vector.memset(stack[1][SR:CR, 1, :, :].bitcast(F32), 1.0).then_inc(memsets, 1)

            def q_low(t, half):
                u = t + 2
                dve.wait_ge(qH_done, 2 * u + half + 1)
                n = slice(512 * half, 512 * half + 512)
                nc.vector.scalar_tensor_tensor(out=parts[:, 1, n], in0=X, scalar=bqk[:, 0:1],
                                               in1=parts[:, 0, n].bitcast(F32), op0=ALU.add,
                                               op1=ALU.subtract).then_inc(qL_done, 1)

            def row_max(t, m):
                j, i, part = MAXES[m]
                v = t + 1
                w = 512 if i >= 4 and part == 0 else 128 * (i + 1) - 512 * part
                dve.wait_ge(max_mm, NM * v + m + 1)
                nc.vector.tensor_reduce(pm[v % 2][:, j, i, part:part + 1], M[m % 2][:, 0:w], AX.X,
                                        ALU.max).then_inc(max_done, 1)

            for t in range(-2, NU):
                v = t + 1
                if 0 <= v < NU:
                    b, g = v // NG, v % NG
                    if v >= 2:
                        dve.wait_ge(pv_mm, NC * (v - 1))
                    nc.vector.tensor_copy(
                        vu[v % 2][:, :, :, 0:HD],
                        vnat[:, NT * b:NT * b + NT, G * HD * g:G * HD * (g + 1)].rearrange(
                            "p t (j e) -> p t j e", e=HD)).then_inc(vu_done, 1)
                for c in range(NC):
                    mine = MAX_STEPS[c] if 0 <= v < NU else []
                    for m in mine[:len(mine) // 2]:
                        row_max(t, m)
                    if t + 2 < NU and c in WQK_STEP:
                        q_low(t, WQK_STEP.index(c))
                    for m in mine[len(mine) // 2:]:
                        row_max(t, m)
                    if 0 <= v < NU and c == NC - 2:
                        dve.wait_ge(max_done, NM * (v + 1))
                        nc.vector.tensor_reduce(nm[:], pm[v % 2][:].rearrange("p j i s -> p (j i) s"), AX.X, ALU.max,
                                                negate=True).then_inc(nm_step, 1)
                        dve.wait_ge(nm_step, 2 * v + 1)
                        nc.vector.tensor_copy(nms[:, 0, :], nm[:]).then_inc(nm_step, 1)
                        dve.wait_ge(nm_step, 2 * v + 2)
                        nc.vector.tensor_tensor(nms[:, 1, :], nm[:], nms[:, 0, :].bitcast(F32),
                                                ALU.subtract).then_inc(nm_done, 1)

            def part_a(i):
                s = i % 2
                dve.wait_ge(tr1, i + 1)
                o = ps[:, 0:4, :].rearrange("p i (h c) -> p (i h) c", c=32)
                then(nc.vector.reciprocal(recd[:, s, :].rearrange("p (n o) -> p n o", o=1), o[:, :, HD:HD + 1]))
                if i >= 2:
                    dve.wait_ge(tr2, i - 1)
                nc.vector.tensor_tensor(ynat[:, s].rearrange("p t (h e) -> p (t h) e", e=HD), o[:, :, 0:HD],
                                        recd[:, s, :].rearrange("p (n o) -> p n o", o=1).to_broadcast([128, 64, HD]),
                                        ALU.mult).then_inc(ynat_done, 1)
                dve.wait_ge(x1_mm, i + 1)
                dve.wait_ge(xadd_done, B)
                nc.vector.tensor_tensor(xs[:, 4 * i:4 * i + 4, :], ps[:, 5, :].rearrange("p (t c) -> p t c", c=C),
                                        xs[:, 4 * i:4 * i + 4, :], ALU.add).then_inc(x1_done, 1)
                dve.wait_ge(x1_done, i + 1)
                norm_stats(i, stats2)
                normalise(i, z2, std2, z2_done)

            def part_b(i):
                b = i // 2
                dve.wait_ge(f2_mm, i + 1)
                nc.vector.tensor_tensor(proc[:, 4 * i:4 * i + 4, :], ps[:, 5, :].rearrange("p (t c) -> p t c", c=C),
                                        bc[:, 5, b:b + 1, :].to_broadcast([128, 4, C]), ALU.add).then_inc(proc_done, 1)

            def rank(b):
                S = srow[:, T * b:T * b + T]
                S3 = S.rearrange("p (t n) -> p t n", n=128)
                dve.wait_ge(srow_done, 2 * (b + 1))
                if b:
                    dve.wait_ge(rank_mm, b)
                sm = smask.rearrange("p (t n) -> p t n", n=128)
                then(nc.vector.tensor_tensor(sm, S3, ident[:].rearrange("p (o n) -> p o n", o=1).to_broadcast(
                    [128, NT, 128]), ALU.mult))
                nc.vector.tensor_reduce(scol[:, NT * b:NT * b + NT], sm, AX.X, ALU.add).then_inc(scol_done, 1)
                dve.wait_ge(scol_done, b + 1)
                if b:
                    dve.wait_ge(gt_done, 22 * b)
                for j in range(NT):
                    blk = slice(128 * j, 128 * (j + 1))
                    ins = nc.vector.scalar_tensor_tensor(out=eqm[:, blk], in0=S[:, blk], scalar=scol[:, NT * b + j:NT * b + j + 1],
                                                         in1=tri[:], op0=ALU.is_equal, op1=ALU.mult)
                then(ins)
                for j in range(NT):
                    sj = scol[:, NT * b + j:NT * b + j + 1]
                    gj, blk = before[j], slice(128 * j, 128 * (j + 1))
                    if j:
                        nc.vector.tensor_scalar(gj[:, 0:128 * j], S[:, 0:128 * j], sj, None, ALU.is_lt).then_inc(gt_done, 1)
                    if j < NT - 1:
                        nc.vector.tensor_scalar(gj[:, 128 * (j + 1):], S[:, 128 * (j + 1):], sj, None,
                                                ALU.is_le).then_inc(gt_done, 1)
                    nc.vector.scalar_tensor_tensor(out=gj[:, blk], in0=S[:, blk], scalar=sj, in1=eqm[:, blk],
                                                   op0=ALU.is_lt, op1=ALU.add).then_inc(gt_done, 1)

            def finish(b):
                dve.wait_ge(rank_mm, b + 1)
                dve.wait_ge(sig_done, b + 1)
                n = slice(NT * b, NT * b + NT)
                then(nc.vector.scalar_tensor_tensor(out=wsel[:, n], in0=ps[:, 6, 0:NT], scalar=float(KEEP),
                                                    in1=sig[:, n], op0=ALU.is_lt, op1=ALU.mult))
                for t in range(NT * b, NT * b + NT):
                    if t % 4 == 0:
                        dve.wait_ge(proc_done, t // 4 + 1)
                        dve.wait_ge(res_done, t // 4 + 1)
                    nc.vector.scalar_tensor_tensor(out=fin[:, t, :], in0=proc[:, t, :], scalar=wsel[:, t:t + 1],
                                                   in1=res[:, t, :], op0=ALU.mult, op1=ALU.add).then_inc(fin_done, 1)

            part_a(0)
            part_a(1)
            part_b(0)
            part_a(2)
            part_b(1)
            rank(0)
            part_a(3)
            finish(0)
            part_b(2)
            part_b(3)
            rank(1)
            finish(1)


        @block.tensor
        def _(pe):
            mm = nc.tensor.matmul

            def transposes(i):
                pe.wait_ge(zn_done, i + 1)
                if i >= 2:
                    pe.wait_ge(hT_done, i - 1)
                for n in range(4):
                    ins = nc.tensor.transpose(ps[:, i % 2, 128 * n:128 * n + 128], zn[:, 4 * i + n, :], ident[:])
                ins.then_inc(zn_tr, 1)

            pe.wait_ge(const_in, 16)
            transposes(0)
            pe.wait_ge(mod_in, 48)
            pe.wait_ge(silu_done, 1)
            for k in range(6):
                ins = mm(ps[:, 6, B * k:B * k + B], wmod[:, 128 * k:128 * k + 128], sig[:, 6:8], start=True, stop=True)
            ins.then_inc(mod_mm, 1)
            pe.wait_ge(qkv_in, 48)
            for i in range(QD):
                if i + 1 < QD:
                    transposes(i + 1)
                n5 = slice(512 * i, 512 * i + 512)
                pe.wait_ge(hT_done, i + 1)
                for a in range(2):
                    if i:
                        pe.wait_ge(qkL_done, 2 * i - 1 + a)
                    mm(ps[:, 2 + a, :], wqkvT[:, 128 * a:128 * a + 128], hT[:, n5], start=True,
                       stop=True).then_inc(qk_mm, 1)
                if i:
                    pe.wait_ge(v_done, i)
                for n in range(4):
                    ins = mm(ps[:, 4, 128 * n:128 * n + 128], hT[:, 512 * i + 128 * n:512 * i + 128 * n + 128],
                             wqkvT[:, 256:384], start=True, stop=True)
                ins.then_inc(v_mm, 1)
            pe.wait_ge(attn_in, 144)
            mm(ps[:, 5, 0:128], l2oT[:], kvrep[:], start=True, stop=True).then_inc(m8_mm, 1)
            pe.wait_ge(gates_done, 1)
            mm(ps[:, 6, 128:129], l2oT[:], kvb[:], start=True, stop=True).then_inc(yb_mm, 1)
            pe.wait_ge(yb_done, 1)
            mm(ps[:, 6, 256:257], cpT[:], yb[:, 0:1], start=True, stop=True).then_inc(yb_mm, 1)
            pe.wait_ge(m8_done, 1)
            pe.wait_ge(v_done, QD)
            mm(ps[:, 4, 0:128], m8[:], cpT[:], start=True, stop=True).then_inc(wo_mm, 1)
            pe.wait_ge(memsets, 2)
            pe.wait_ge(diag_done, 1)
            flat = diag.rearrange("p r b c -> p (r b c)")
            for n in range(3):
                mm(ps[:, 5 + n, :], ones[:], flat[:, 512 * n:512 * n + 512], start=True, stop=True).then_inc(bc_mm, 1)
            pe.wait_ge(bc_done, 3)
            pe.wait_ge(wo_done, 2)
            pe.wait_ge(wsplit_done, 2)
            pe.wait_ge(memsets, 10)

            def x_free(u, last):
                kind, n = last
                if kind == "proj":
                    pe.wait_ge(proj_ev, 8 * u + n + 1)
                elif kind == "wqk":
                    pe.wait_ge(qH_done, 2 * u + n + 1)
                    pe.wait_ge(qL_done, 2 * u + n + 1)
                else:
                    pe.wait_ge(nmT_done, u + 1)

            def project(t, n):
                a, half, rot = PROJ[n]
                u = t + 2
                if n == 0:
                    pe.wait_ge(s8_in, 48 * (u + 1))
                mm(X, wsplit[:, 2 * a + rot, :], s8[:, a, 512 * half:512 * half + 512], start=True,
                   stop=True).then_inc(proj_mm, 1)

            def map_q(t, half):
                u = t + 2
                pe.wait_ge(rope_done, 4 * u + half + 1)
                mm(X, wqk[:], rope[:, 0, 512 * half:512 * half + 512], start=True, stop=True).then_inc(wqk_mm, 1)

            def max_scores(t, m):
                j, i, part = MAXES[m]
                v = t + 1
                st = stack[v % 2]
                k0 = 512 * part
                w = 512 if i >= 4 and part == 0 else 128 * (i + 1) - k0
                diagonal = k0 + w == 128 * (i + 1)
                if i == 0:
                    pe.wait_ge(head_in[j], 48 * (v + 1))
                if NM * v + m >= 2:
                    pe.wait_ge(max_done, NM * v + m - 1)
                bank = M[m % 2]
                ins = mm(bank[:, 0:w], st[0:SR, 0, j, 128 * i:128 * i + 128], st[0:SR, 1, j, k0:k0 + w],
                         start=True, stop=not diagonal)
                if diagonal:
                    ins = mm(bank[:, w - 128:w], identb[:], maskb[:], start=False, stop=True)
                ins.then_inc(max_mm, 1)

            def scores(t, c, pair):
                q, k, off, w = CHUNKS[c]
                st = stack[t % 2]
                if NC * t + c >= 1:
                    pe.wait_ge(exp_done, 2 * NC * t + 2 * (c - 1) + pair + 1)
                for n in range(2):
                    j = 2 * pair + n
                    ins = mm(E[pair][:, n, 0:w], st[0:CR, 1, j, 128 * k:128 * k + 128],
                             st[0:CR, 0, j, 512 * q + off:512 * q + 512], start=True, stop=True)
                ins.then_inc(score_mm, 1)

            def values(t, c):
                q, k, off, w = CHUNKS[c]
                if c in DIAG:
                    pe.wait_ge(sel_done, len(DIAG) * t + DIAG.index(c) + 1)
                else:
                    pe.wait_ge(exp_done, 2 * NC * t + 2 * c + 2)
                if k == 0 and 2 * t + q > 0:
                    pe.wait_ge(o_done, 2 * t + q)
                for j in range(G):
                    ins = mm(O[32 * j:32 * j + 32, off:512], vu[t % 2][:, k, j, :], probs[:, c % RING, j, 0:w],
                             start=(k == 0), stop=(c in LAST), skip_group_check=True)
                ins.then_inc(pv_mm, 1)

            for t in range(-2, NU):
                softmax, maxima, prep = t >= 0, 0 <= t + 1 < NU, t + 2 < NU
                last = ("max", t) if t >= 0 else ("proj", 7) if t == -1 else None
                last_unit = t if t >= 0 else 0
                if softmax:
                    pe.wait_ge(row_in, 32 * (t + 1))
                    pe.wait_ge(vu_done, t + 1)
                for c in range(NC):
                    mine = MAX_STEPS[c] if maxima else []
                    if softmax:
                        scores(t, c, 0)
                    for m in mine[:len(mine) // 2]:
                        max_scores(t, m)
                    if softmax:
                        scores(t, c, 1)
                    if prep and c in WQK_STEP:
                        x_free(last_unit, last)
                        map_q(t, WQK_STEP.index(c))
                        last, last_unit = ("wqk", WQK_STEP.index(c)), t + 2
                    if prep and c in PROJ_STEP:
                        n = PROJ_STEP.index(c)
                        if last:
                            x_free(last_unit, last)
                        project(t, n)
                        last, last_unit = ("proj", n), t + 2
                    for m in mine[len(mine) // 2:]:
                        max_scores(t, m)
                    if softmax and c >= LAG:
                        values(t, c - LAG)
                if softmax:
                    values(t, NC - 2)
                if maxima:
                    v = t + 1
                    if last:
                        x_free(last_unit, last)
                    pe.wait_ge(nm_done, v + 1)
                    nc.tensor.transpose(ps[0:64, 7, 0:128], nms[:].bitcast(F32).rearrange("p s n -> p (s n)"),
                                        ident[:]).then_inc(nm_tr, 1)
                if softmax:
                    values(t, NC - 1)

            def part_a(i, f1s, f2s):
                b, s = i // 2, i % 2
                if i == 0:
                    pe.wait_ge(o_done, 2 * NU)
                if f1s:
                    pe.wait_ge(gelu_done, FT * f1s)
                for n in range(4):
                    for g in range(NG):
                        n0 = 512 * (i % 2) + 128 * n
                        ins = nc.tensor.transpose(ps[:, n, 128 * g:128 * g + 128], oT[:, NG * b + g, n0:n0 + 128],
                                                  ident[:])
                ins.then_inc(tr1, 1)
                pe.wait_ge(ynat_done, i + 1)
                if i:
                    pe.wait_ge(yT_done, i)
                for n in range(4):
                    ins = nc.tensor.transpose(ps[:, 4, 128 * n:128 * n + 128], ynat[:, s, n, :], ident[:])
                ins.then_inc(tr2, 1)
                pe.wait_ge(yT_done, i + 1)
                if i:
                    pe.wait_ge(x1_done, i)
                if f2s:
                    pe.wait_ge(proc_done, f2s)
                for n in range(4):
                    ins = mm(ps[:, 5, 128 * n:128 * n + 128], yT[:, s, 128 * n:128 * n + 128], woT[:, b, :],
                             start=True, stop=True)
                ins.then_inc(x1_mm, 1)

            def part_b(i, tr1s):
                b, s = i // 2, i % 2
                pe.wait_ge(z2_done, i + 1)
                if i:
                    pe.wait_ge(h2T_done, i)
                if i == 2:
                    pe.wait_ge(fin_done, 1)
                for n in range(4):
                    ins = nc.tensor.transpose(ps[:, 6, 128 * n:128 * n + 128], z2[:, 4 * i + n, :], ident[:])
                ins.then_inc(tr3, 1)
                n5 = slice(512 * i, 512 * i + 512)
                pe.wait_ge(h2T_done, i + 1)
                if i:
                    pe.wait_ge(srow_done, i)
                pe.wait_ge(ffn_in, 64)
                mm(ps[:, 7, :], wrb[:], h2T[:, n5], start=True, stop=True).then_inc(sc_mm, 1)
                pe.wait_ge(ynat_done, tr1s)
                for f in range(FT):
                    if i:
                        pe.wait_ge(gelu_done, FT * (i - 1) + f + 1)
                    mm(ps[:, f, :], w1[:, 128 * f:128 * f + 128], h2T[:, n5], start=True,
                       stop=True).then_inc(f1_mm, 1)
                pe.wait_ge(gelu_done, FT * (i + 1))
                pe.wait_ge(w2g_done, B)
                pe.wait_ge(x1_done, tr1s)
                if i:
                    pe.wait_ge(proc_done, i)
                for n in range(4):
                    for f in range(FT):
                        ins = mm(ps[:, 5, 128 * n:128 * n + 128], actT[:, s, f, 128 * n:128 * n + 128],
                                 w2g[:, b, f, :], start=(f == 0), stop=(f == FT - 1))
                ins.then_inc(f2_mm, 1)

            def rank(b):
                pe.wait_ge(gt_done, 22 * (b + 1))
                pe.wait_ge(h2T_done, 2 * (b + 1))
                for i in range(NT):
                    for j in range(NT):
                        ins = mm(ps[:, 6, i:i + 1], before[j][:, 128 * i:128 * i + 128], onesb[:, 0:1],
                                 start=(j == 0), stop=(j == NT - 1))
                ins.then_inc(rank_mm, 1)

            part_a(0, 0, 0)
            part_a(1, 0, 0)
            part_b(0, 2)
            part_a(2, 1, 1)
            part_b(1, 3)
            part_a(3, 2, 2)
            rank(0)
            part_b(2, 4)
            part_b(3, 4)
            rank(1)


def lay_out(i):
    f = {k: np.asarray(v) for k, v in i.items()}
    cols = np.zeros((128, 16), np.float32)
    wc, bcn = f["L0_attn_c_attn_w"], f["L0_attn_c_attn_b"]
    swap = np.arange(L) ^ 1
    cols[:, 0], cols[:, 1] = bcn[0:C], bcn[C:2 * C]
    cols[:, 2] = np.tile(f["L0_attn_q2l_b"], G)
    cols[:, 3] = np.tile(f["L0_attn_q2l_b"][swap], G)
    cols[:, 4] = np.tile(f["L0_attn_kv2l_b"], G)
    cols[:, 5] = np.tile(f["L0_attn_kv2l_b"][swap], G)
    cols[:, 6] = np.tile(f["L0_attn_wqk_b"], G)
    cols[:, 7] = np.tile(f["L0_attn_l2o_b"], H)
    cols[:, 8] = f["L0_attn_cproj_b"]
    cols[:, 9] = f["L0_ffn_b2"]
    cols[:, 10:10 + FT] = f["L0_ffn_b1"].reshape(FT, 128).T
    wlat = np.zeros((3, G, HD, 4, G, L), np.float32)
    wqk = np.zeros((G, L, G, L), np.float32)
    for j in range(G):
        for k, w in enumerate((f["L0_attn_q2l_w"], f["L0_attn_q2l_w"][swap],
                               f["L0_attn_kv2l_w"], f["L0_attn_kv2l_w"][swap])):
            wlat[:, j, :, k, j, :] = w.T
        wqk[j, :, j, :] = f["L0_attn_wqk_w"].T
    inv = (np.float32(1.0) / np.float32(10000.0) ** (np.arange(0, L, 2, dtype=np.float32) / np.float32(L)))
    ang = np.repeat(np.outer(np.arange(T, dtype=np.float32), inv.astype(np.float32)), 2, axis=1).astype(np.float32)
    sign = np.where(np.arange(L) % 2 == 0, -1.0, 1.0)
    cos = np.tile(np.cos(ang.astype(np.float64)).T, (G, 1)).astype(np.float32)
    sin = np.tile((np.sin(ang.astype(np.float64)) * sign).T, (G, 1)).astype(np.float32)
    at = np.arange(128)
    return {
        "x": f["L0_attn_x"], "ident": np.eye(128, dtype=np.float32),
        "tri": (at[None, :] > at[:, None]).astype(np.float32),
        "blockd": (at[None, :] // HD == at[:, None] // HD).astype(np.float32),
        "cos": cos, "sin": sin, "cT": f["L0_c"].T, "wmod": f["L0_wmod"], "cols": cols,
        "wqkvT": wc.T, "bv": np.broadcast_to(bcn[2 * C:], (128, C)), "wlat": wlat.reshape(SR, 4, 128),
        "wqk": wqk.reshape(128, 128), "cpT": f["L0_attn_cproj_w"].T,
        "l2oT": np.tile(f["L0_attn_l2o_w"].T, (1, H)), "kvrep": np.tile(f["L0_attn_kv2l_w"], (1, H)),
        "kvb": f["L0_attn_kv2l_b"].reshape(L, 1), "w1": f["L0_ffn_W1"],
        "w2": f["L0_ffn_W2"].reshape(FT, 128, C).transpose(1, 0, 2),
        "wr": np.broadcast_to(f["L0_ffn_w_router"][:, None], (C, 128)),
    }


def kernel(**inputs):
    import concourse.bacc as bacc
    from concourse.bass_utils import run_bass_kernel_spmd

    nc = bacc.Bacc("TRN2", target_bir_lowering=False, num_devices=1)
    arrays, d = {}, {}
    for name, a in lay_out(inputs).items():
        a = np.ascontiguousarray(a)
        arrays[f"in_{name}"] = a
        d[name] = nc.dram_tensor(f"in_{name}", a.shape, mybir.dt.from_np(a.dtype), kind="ExternalInput").ap()
    out = nc.dram_tensor("out_x", (B, T, C), F32, kind="ExternalOutput").ap()
    adaln_block(nc, d, out)
    r = run_bass_kernel_spmd(nc, [arrays], core_ids=[0])
    return r.results[0]["out_x"]
```

```python
from contextlib import ExitStack

import numpy as np
import concourse.bass as bass
from concourse import mybir

F32 = mybir.dt.float32
F32R = mybir.dt.float32r
BF16 = mybir.dt.bfloat16
ACT = mybir.ActivationFunctionType
ALU = mybir.AluOpType
AX = mybir.AxisListType

B, T, C = 2, 1024, 128
H, HD, L = 16, 8, 32
F = 512
KEEP = T // 2
G = 4
NG = H // G
NU = B * NG
NT = T // 128
QD = B * T // 512
FT = F // 128
SR = 3 * L
NEG = -3.0e38
MASKED = -1.0e30
EPS = 1e-5

HALVES = [1, 0]
CHUNKS = [(ph, q, k, max(0, 128 * k - 512 * q), 512 - max(0, 128 * k - 512 * q))
          for ph, q in enumerate(HALVES) for k in range(4 * (q + 1))]
NC = len(CHUNKS)
DIAG = [n for n, (_, q, k, _, _) in enumerate(CHUNKS) if 128 * k >= 512 * q]
LAST = [max(n for n in range(NC) if CHUNKS[n][0] == ph) for ph in range(2)]


def max_width(i, part):
    return min(512, 128 * (i + 1) - 512 * part)


MAXES = [(ph, i, part, j, max(1, min(G, 512 // max_width(i, part))))
         for ph, q in enumerate(HALVES) for part in range(q, -1, -1) for i in range(4 * q, 4 * q + 4)
         for j in range(0, G, max(1, min(G, 512 // max_width(i, part))))]
NM = len(MAXES)
RING = 3
LAG = 2
FIRST_MAX = 1


PROJ = [(a, half, rot) for a in range(2) for half in HALVES for rot in range(2)]
JOBS = {(0, 0): ("proj", 0), (0, 1): ("proj", 1), (1, 0): ("proj", 2), (1, 1): ("proj", 3),
        (2, 0): ("wqk", 0), (2, 1): ("proj", 4), (3, 0): ("proj", 5), (4, 0): ("wqk", 1),
        (4, 1): ("proj", 6), (5, 0): ("proj", 7)}
ROPE_STEP = {1: (0, 1), 2: (0, 0), 3: (1, 1), 5: (1, 0)}
KH_STEP = {5: 1, 7: 0}
KL_STEP = {6: 1, 8: 0}


def plan():
    act = [4 * w + 4 * 100 + sum(650 for p in range(2) if (c, p) in JOBS) + 600 * (c in KH_STEP) +
           600 * (c in COPY_STEP) for c, (_, _, _, _, w) in enumerate(CHUNKS)]
    cost = [max_width(i, part) * n + 90 for _, i, part, _, n in MAXES]
    steps, m, at, phases = [], 0, 0, 0
    for c in range(NC):
        mine = []
        while m < NM and c >= FIRST_MAX and \
                at + cost[m] / 2 < sum(cost) * sum(act[FIRST_MAX:c + 1]) / sum(act[FIRST_MAX:]):
            at += cost[m]
            mine.append(("max", m))
            m += 1
        order = []
        for left, rest in ((4, [("scores", 0)]), (3, [JOBS.get((c, 0)), ("scores", 1)]),
                           (2, [("values", 0)]), (1, [JOBS.get((c, 1))])):
            share = -(-len(mine) // left)
            order += mine[:share] + [x for x in rest if x]
            mine = mine[share:]
        if phases < 2 and (c == NC - 1 or m > NM_END[phases] + 3):
            order.append(("turn", phases))
            phases += 1
        steps.append(order)
    return steps


COPY_STEP = [(LAST[ph] + LAG + 1) % NC for ph in range(2)]
NM_END = [max(m for m in range(NM) if MAXES[m][0] == ph) + 1 for ph in range(2)]
STEPS = plan()
BANKED = [x for order in STEPS for x in order if x[0] not in ("scores", "values")]


def adaln_block(nc, d, out):
    with ExitStack() as ctx:
        def sb(name, shape, dt=F32):
            return ctx.enter_context(nc.sbuf_tensor(name, shape, dt))

        def sem(name):
            return ctx.enter_context(nc.semaphore(name))

        xs = sb("xs", [128, B * NT, C])
        ident = sb("ident", [128, 128])
        identb = sb("identb", [128, 128], BF16)
        maskb = sb("maskb", [128, 128], BF16)
        ones = sb("ones", [128, 128])
        cosT = sb("cosT", [128, T])
        sinT = sb("sinT", [128, T])
        cT = sb("cT", [128, B])
        cols = sb("cols", [128, 16])
        wsplit = sb("wsplit", [SR, 4, 128], F32R)
        wqk = sb("wqk", [128, 128])
        bqk = sb("bqk", [128, 1])
        cpT = sb("cpT", [128, C])
        kvb = sb("kvb", [L, 1])
        tri = sb("tri", [128, 128])
        wrb = sb("wrb", [128, 128])
        bvb = sb("bvb", [128, C])
        w1 = sb("w1", [128, F])
        w2g = sb("w2g", [128, B, FT, C])
        woT = sb("woT", [128, B, C])
        bc = sb("bc", [128, 6, B, C])
        modc = sb("modc", [128, 6, B])
        gate = sb("gate", [128, 10, B])
        yb = sb("yb", [128, 4])
        vnat = sb("vnat", [128, B * NT, C])
        vu = [sb(f"vu{p}", [128, NT, G, 32]) for p in range(2)]
        parts = sb("parts", [128, 4, T], F32R)
        rope = sb("rope", [128, 2, T])
        s8 = sb("s8", [SR, 2, T], F32R)
        probs = sb("probs", [128, RING, G, 512])
        oT = sb("oT", [128, NU, T])
        pm = [sb(f"pm{p}", [128, 2, 4, G, 2]) for p in range(2)]
        nm = sb("nm", [128, 2, 4, G])
        nms = sb("nms", [128, 2, 4, 2, G], F32R)
        nmT_both = sb("nmT", [64, 512])
        nmT = [nmT_both[0:2 * G], nmT_both[32:32 + 2 * G]]
        bst = sb("bst", [128, B * NT, 6])
        mv = sb("mv", [128, B * NT, 2])
        std = sb("std", [128, B * NT])
        rstd = sb("rstd", [128, B * NT])
        epsc = sb("epsc", [128, 1])
        onesb = sb("onesb", [128, 2], BF16)
        scol = sb("scol", [128, B * NT])
        wsel = sb("wsel", [128, B * NT])
        sig = sb("sig", [128, B * NT])

        with ExitStack() as shared:
            stack = [shared.enter_context(nc.sbuf_tensor(f"stack{p}", [128, 2, G, T], F32R))
                     for p in range(2)]
        late, late2 = sb("late", [128, 2 * G * T]), sb("late2", [128, 2 * G * T])

        early = oT[:].rearrange("p u t -> p (u t)")
        hT = early[:, 0:2048]
        zn = early[:, 2048:4096].rearrange("p (t c) -> p t c", c=C)
        wmod = early[:, 4096:4864]
        wqkvT = early[:, 4864:5248]
        diag = early[:, 5248:6784].rearrange("p (r b c) -> p r b c", r=6, b=B)
        wraw = early[0:SR, 6784:7296].rearrange("p (k m) -> p k m", k=4)
        blockd, m8 = early[:, 7296:7424], early[:, 7424:7552]
        kvrep, l2oT = early[0:L, 7552:7680], early[0:L, 7680:7808]
        whi = parts[0:SR, 0, 0:512].rearrange("p (k m) -> p k m", k=4)
        q8 = stack[1][:].rearrange("p a j t -> p (a j t)").rearrange("p (k n) -> p k n", k=4)
        ynat = late[:, 0:1024].rearrange("p (s t c) -> p s t c", s=2, c=C)
        yT = late[:, 1024:2048].rearrange("p (s n) -> p s n", s=2)
        z2 = late[:, 2048:4096].rearrange("p (t c) -> p t c", c=C)
        h2T = late[:, 4096:6144]
        srow = late[:, 6144:8192]
        actT = late2[:, 0:4096].rearrange("p (s f n) -> p s f n", s=2, f=FT)
        res = late2[:, 4096:6144].rearrange("p (t c) -> p t c", c=C)
        proc = late2[:, 6144:8192].rearrange("p (t c) -> p t c", c=C)
        lateP = probs[:].rearrange("p r j n -> p (r j n)")
        smask = lateP[:, 0:1024]
        fin = lateP[:, 1024:3072].rearrange("p (t c) -> p t c", c=C)
        eqm = lateP[:, 3072:4096]
        recd = lateP[:, 4096:4224].rearrange("p (s n) -> p s n", s=2)
        before = [rope[:, n // 2, :].bitcast(BF16)[:, T * (n % 2):T * (n % 2) + T] for n in range(4)] + \
                 [t[:].bitcast(BF16)[:, T * n:T * n + T] for t in (cosT, sinT) for n in range(2)]

        ps = ctx.enter_context(nc.psum_tensor("ps", [128, 8, 512], F32))
        E = [ps[:, 0:2, :], ps[:, 2:4, :]]
        O = ps[:, 6, :]

        def work(kind, n):
            return (4, 5, 7)[BANKED.index((kind, n)) % 3]

        x_in = [sem(f"x_in{i}") for i in range(QD)]
        mod_in, qkv_in, attn_in, ffn_in, const_in = (sem(n) for n in (
            "mod_in", "qkv_in", "attn_in", "ffn_in", "const_in"))
        memsets = sem("memsets")
        silu_e, silu_done, mod_mm, mod_done = (sem(n) for n in ("silu_e", "silu_done", "mod_mm", "mod_done"))
        gates_done, diag_done, bc_mm, bc_done = (sem(n) for n in ("gates_done", "diag_done", "bc_mm", "bc_done"))
        m8_mm, m8_done, yb_mm, yb_done, wo_mm, wo_done = (sem(n) for n in (
            "m8_mm", "m8_done", "yb_mm", "yb_done", "wo_mm", "wo_done"))
        dve_step = sem("dve_step")
        stats, std_done, zn_done, zn_tr, hT_done = (sem(n) for n in (
            "stats", "std_done", "zn_done", "zn_tr", "hT_done"))
        qk_mm, qkH_done, qkL_done, v_mm, v_done = (sem(n) for n in (
            "qk_mm", "qkH_done", "qkL_done", "v_mm", "v_done"))
        wsplit_done, xadd_done, w2g_done = (sem(n) for n in ("wsplit_done", "xadd_done", "w2g_done"))
        q8_out, s8_in = [sem(f"q8_out{b}") for b in range(B)], sem("s8_in")
        proj_mm, proj_ev, rope_done, rope_step = (sem(n) for n in ("proj_mm", "proj_ev", "rope_done", "rope_step"))
        wqk_mm, qH_done, qL_done, kH_done, kL_done = (sem(n) for n in (
            "wqk_mm", "qH_done", "qL_done", "kH_done", "kL_done"))
        half_in = [sem(f"half_in{h}") for h in range(2)]
        row_in, vu_done = [sem(f"row_in{h}") for h in range(2)], sem("vu_done")
        tails = sem("tails")
        max_mm, max_done, nm_step, nm_done, nm_tr, nmT_done = (sem(n) for n in (
            "max_mm", "max_done", "nm_step", "nm_done", "nm_tr", "nmT_done"))
        score_mm, exp_done, sel_done, pv_mm, o_done = (sem(n) for n in (
            "score_mm", "exp_done", "sel_done", "pv_mm", "o_done"))
        tr1, rec_done, ynat_done, tr2, yT_done, x1_mm, x1_done = (sem(n) for n in (
            "tr1", "rec_done", "ynat_done", "tr2", "yT_done", "x1_mm", "x1_done"))
        stats2, std2, z2_done, tr3, h2T_done, sc_mm, srow_done = (sem(n) for n in (
            "stats2", "std2", "z2_done", "tr3", "h2T_done", "sc_mm", "srow_done"))
        f1_mm, gelu_done, f2_mm, proc_done, res_step, res_done = (sem(n) for n in (
            "f1_mm", "gelu_done", "f2_mm", "proc_done", "res_step", "res_done"))
        scol_done, gt_done, rank_mm, sig_done, fin_done, out_done = (sem(n) for n in (
            "scol_done", "gt_done", "rank_mm", "sig_done", "fin_done", "out_done"))

        scratch = nc.dram_tensor("q8_scratch", [128, 4, B * T], F32, kind="Internal").ap()

        block = ctx.enter_context(nc.Block())

        CA, SA, CB, SBC, GA, GAO, GB, GBC, GBS, GB2 = range(10)
        ROWS = [GA, GAO, GB, GBC, GBS, GB2]
        BQ, BK, QB, QRB, KB, KRB, WB, LOB, CPB, B2 = range(10)
        B1 = 10

        @block.sync
        def _(sp):
            xd = d["x"].rearrange("b (t p) c -> p (b t) c", p=128)
            for i in range(QD):
                sp.dma_start(xs[:, 4 * i:4 * i + 4, :], xd[:, 4 * i:4 * i + 4, :]).then_inc(x_in[i], 16)
                if i == 0:
                    sp.dma_start(ident[:], d["ident"]).then_inc(const_in, 16)
            sp.dma_start(cosT[:], d["cos"]).then_inc(attn_in, 16)
            sp.dma_start(sinT[:], d["sin"]).then_inc(attn_in, 16)
            for dst, name in ((w1[:], "w1"), (w2g[:, 0], "w2"), (w2g[:, 1], "w2"), (wrb[:], "wr")):
                sp.dma_start(dst, d[name]).then_inc(ffn_in, 16)
            for b in range(B):
                sp.wait_ge(qkH_done, 4 * (b + 1))
                sp.wait_ge(qkL_done, 4 * (b + 1))
                sp.dma_start(scratch[:, :, b * T:(b + 1) * T],
                             q8[:, :, b * T:(b + 1) * T].bitcast(F32)).then_inc(q8_out[b], 16)

            def load_s8(u):
                b, g = (u // NG, u % NG)
                for s, part in enumerate((0, 1, 0)):
                    src = scratch[g * 32:(g + 1) * 32, part::2, b * T:(b + 1) * T]
                    sp.dma_start(s8[s * 32:(s + 1) * 32, :, :].bitcast(F32), src).then_inc(s8_in, 16)

            def load_half(u, half):
                n, ph = slice(512 * half, 512 * half + 512), HALVES.index(half)
                for done in (qH_done, qL_done, kH_done, kL_done):
                    sp.wait_ge(done, 2 * u + ph + 1)
                if u >= 2:
                    sp.wait_ge(score_mm, 2 * (NC * (u - 2) + LAST[ph] + 1))
                if u == 1:
                    for b in range(B):
                        sp.wait_ge(q8_out[b], 16)
                for a, rows in ((0, (0, 1, 0)), (1, (2, 2, 3))):
                    for s, part in enumerate(rows):
                        sp.dma_start(stack[u % 2][s * 32:(s + 1) * 32, a, :, n].bitcast(F32),
                                     parts[:, part, n].bitcast(F32)).then_inc(half_in[half], 16)

            def load_rows(u, half):
                sp.wait_ge(nmT_done, 2 * u + HALVES.index(half) + 1)
                if u <= 1:
                    sp.wait_ge(tails, 2 * u + 2)
                for hl in range(2):
                    row = stack[u % 2][SR + hl:SR + hl + 1, 0, :, 512 * half:512 * half + 512].bitcast(F32)
                    sp.dma_start(row, nmT[half][hl * G:(hl + 1) * G, :]).then_inc(row_in[half], 16)

            sp.wait_ge(q8_out[0], 16)
            load_s8(0)
            for t in range(-2, NU):
                if t + 3 < NU:
                    sp.wait_ge(proj_mm, 8 * (t + 3))
                    if t + 3 == NG:
                        sp.wait_ge(q8_out[1], 16)
                    load_s8(t + 3)
                for half in HALVES:
                    if 0 <= t + 1 < NU:
                        load_rows(t + 1, half)
                    if t + 2 < NU:
                        load_half(t + 2, half)
            od = out.rearrange("b (t p) c -> p (b t) c", p=128)
            for i in range(QD):
                sp.wait_ge(fin_done, 4 * (i + 1))
                sp.dma_start(od[:, 4 * i:4 * i + 4, :], fin[:, 4 * i:4 * i + 4, :]).then_inc(out_done, 16)
            sp.wait_ge(out_done, 16 * QD)

        @block.scalar
        def _(act):
            for dst, name in ((cT[:], "cT"), (wmod, "wmod"), (cols[:], "cols")):
                act.dma_start(dst, d[name]).then_inc(mod_in, 16)
            for dst, name in ((wqkvT, "wqkvT"), (bvb[:], "bv"), (wraw, "wlat")):
                act.dma_start(dst, d[name]).then_inc(qkv_in, 16)
            for dst, name in ((wqk[:], "wqk"), (cpT[:], "cpT"), (l2oT[:], "l2oT"), (kvrep[:], "kvrep"),
                              (kvb[:], "kvb"), (blockd[:], "blockd"), (tri[:], "tri")):
                act.dma_start(dst, d[name]).then_inc(attn_in, 16)
            act.wait_ge(mod_in, 48)
            nc.scalar.activation(sig[:, 0:B], cT[:], ACT.Exp, scale=-1.0).then_inc(silu_e, 1)
            act.wait_ge(memsets, 1)
            for i in range(QD):
                act.wait_ge(stats, 4 * (i + 1))
                nc.scalar.activation(std[:, 4 * i:4 * i + 4], mv[:, 4 * i:4 * i + 4, 1], ACT.Sqrt,
                                     bias=epsc[:, 0:1]).then_inc(std_done, 1)

            def qk_high(i, a):
                act.wait_ge(qk_mm, 2 * i + a + 1)
                nc.scalar.activation(q8[:, 2 * a, 512 * i:512 * i + 512], ps[:, 2 + a, :], ACT.Identity,
                                     bias=cols[:, BQ + a:BQ + a + 1]).then_inc(qkH_done, 1)

            act.wait_ge(gates_done, 4)
            for i in range(QD):
                b = i // 2
                act.wait_ge(zn_tr, i + 1)
                nc.scalar.activation(hT[:, 512 * i:512 * i + 512], ps[:, i % 2, :], ACT.Identity,
                                     bias=gate[:, SA, b:b + 1], scale=gate[:, CA, b:b + 1]).then_inc(hT_done, 1)
                if i:
                    qk_high(i - 1, 0)
                    qk_high(i - 1, 1)
            qk_high(QD - 1, 0)
            qk_high(QD - 1, 1)
            for n in range(3):
                act.wait_ge(bc_mm, n + 1)
                nc.scalar.copy(bc[:].rearrange("p r b c -> p (r b c)")[:, 512 * n:512 * n + 512],
                               ps[:, 5 + n, :]).then_inc(bc_done, 1)

            def projected(t, n):
                a, half, rot = PROJ[n]
                u, ph = t + 2, HALVES.index(half)
                act.wait_ge(proj_mm, 8 * u + n + 1)
                if a == 0 and u > 0:
                    act.wait_ge(kH_done, 2 * u - 1 + ph)
                    act.wait_ge(kL_done, 2 * u - 1 + ph)
                if a == 1:
                    act.wait_ge(wqk_mm, 2 * u + ph + 1)
                bias = cols[:, QB + 2 * a + rot:QB + 2 * a + rot + 1]
                nc.scalar.activation(rope[:, rot, 512 * half:512 * half + 512], ps[:, work("proj", n), :], ACT.Identity,
                                     bias=bias).then_inc(proj_ev, 1)

            def q_high(t, ph):
                u, half = t + 2, HALVES[ph]
                act.wait_ge(wqk_mm, 2 * u + ph + 1)
                if u >= 1:
                    act.wait_ge(half_in[half], 96 * u)
                nc.scalar.activation(parts[:, 0, 512 * half:512 * half + 512], ps[:, work("wqk", ph), :], ACT.Identity,
                                     bias=bqk[:, 0:1]).then_inc(qH_done, 1)

            def k_high(t, half):
                u = t + 2
                act.wait_ge(rope_done, 4 * u + 2 + HALVES.index(half) + 1)
                if u >= 1:
                    act.wait_ge(half_in[half], 96 * u)
                nc.scalar.copy(parts[:, 2, 512 * half:512 * half + 512],
                               rope[:, 0, 512 * half:512 * half + 512]).then_inc(kH_done, 1)

            def exps(t, c, pair):
                _, q, k, off, w = CHUNKS[c]
                act.wait_ge(score_mm, 2 * NC * t + 2 * c + pair + 1)
                if NC * t + c >= RING:
                    act.wait_ge(pv_mm, NC * t + c - RING + 1)
                nc.scalar.activation(probs[:, c % RING, 2 * pair:2 * pair + 2, 0:w], E[pair][:, :, 0:w],
                                     ACT.Exp).then_inc(exp_done, 1)

            def turned(v, ph):
                act.wait_ge(nm_tr, 2 * v + ph + 1)
                if v >= 1:
                    act.wait_ge(row_in[HALVES[ph]], 32 * v)
                nc.scalar.copy(nmT[HALVES[ph]], ps[0:2 * G, work("turn", ph), :]).then_inc(nmT_done, 1)

            def o_copy(t, ph):
                q = HALVES[ph]
                act.wait_ge(pv_mm, NC * t + LAST[ph] + 1)
                nc.scalar.copy(oT[:, t, 512 * q:512 * q + 512], O).then_inc(o_done, 1)

            act.wait_ge(attn_in, 144)
            for t in range(-2, NU):
                for c in range(NC):
                    for kind, n in STEPS[c]:
                        if kind == "scores" and t >= 0:
                            exps(t, c, n)
                            if n == 0 and c == COPY_STEP[0]:
                                o_copy(t, 0)
                            if n == 0 and c == COPY_STEP[1] and t >= 1:
                                o_copy(t - 1, 1)
                        elif kind == "proj" and t + 2 < NU:
                            projected(t, n)
                        elif kind == "wqk" and t + 2 < NU:
                            q_high(t, n)
                        elif kind == "turn" and 0 <= t + 1 < NU:
                            turned(t + 1, n)
                    if c in KH_STEP and t + 2 < NU:
                        k_high(t, KH_STEP[c])
            o_copy(NU - 1, 1)

            def part_a(i):
                s = i % 2
                act.wait_ge(tr2, i + 1)
                if i >= 2:
                    act.wait_ge(x1_mm, i - 1)
                nc.scalar.copy(yT[:, s, :], ps[:, 4, :]).then_inc(yT_done, 1)
                act.wait_ge(stats2, 4 * (i + 1))
                nc.scalar.activation(std[:, 4 * i:4 * i + 4], mv[:, 4 * i:4 * i + 4, 1], ACT.Sqrt,
                                     bias=epsc[:, 0:1]).then_inc(std2, 1)

            def part_b(i):
                b, s = i // 2, i % 2
                act.wait_ge(tr3, i + 1)
                nc.scalar.activation(h2T[:, 512 * i:512 * i + 512], ps[:, 6, :], ACT.Identity,
                                     bias=gate[:, SBC, b:b + 1], scale=gate[:, CB, b:b + 1]).then_inc(h2T_done, 1)
                act.wait_ge(sc_mm, i + 1)
                nc.scalar.copy(srow[:, 512 * i:512 * i + 512], ps[:, 7, :]).then_inc(srow_done, 1)
                for f in range(FT):
                    act.wait_ge(f1_mm, FT * i + f + 1)
                    if i >= 2:
                        act.wait_ge(f2_mm, i - 1)
                    nc.scalar.activation(actT[:, s, f, :], ps[:, f, :], ACT.Gelu_apprx_tanh,
                                         bias=cols[:, B1 + f:B1 + f + 1]).then_inc(gelu_done, 1)

            def weights(b):
                act.wait_ge(scol_done, b + 1)
                nc.scalar.activation(sig[:, NT * b:NT * b + NT], scol[:, NT * b:NT * b + NT],
                                     ACT.Sigmoid).then_inc(sig_done, 1)

            part_a(0)
            part_a(1)
            part_b(0)
            part_a(2)
            part_b(1)
            weights(0)
            part_a(3)
            part_b(2)
            part_b(3)
            weights(1)

        @block.gpsimd
        def _(pool):
            nc.gpsimd.memset(stack[0][SR:128].bitcast(F32), 0.0).then_inc(tails, 1)
            pool.wait_ge(tails, 1)
            nc.gpsimd.memset(stack[0][SR:SR + 2, 1].bitcast(F32), 1.0).then_inc(tails, 1)
            pool.wait_ge(tails, 2)
            pool.wait_ge(zn_done, QD)
            pool.wait_ge(bc_done, 3)
            for b in range(B):
                nc.gpsimd.tensor_tensor(xs[:, NT * b:NT * b + NT, :], xs[:, NT * b:NT * b + NT, :],
                                        bc[:, 1, b:b + 1, :].to_broadcast([128, NT, C]), ALU.add).then_inc(xadd_done, 1)
            pool.wait_ge(ffn_in, 64)
            for b in range(B):
                nc.gpsimd.tensor_tensor(w2g[:, b], w2g[:, b], bc[:, 2, b:b + 1, :].to_broadcast([128, FT, C]),
                                        ALU.mult).then_inc(w2g_done, 1)
            for b in range(B):
                pool.wait_ge(q8_out[b], 16)
            pool.wait_ge(w2g_done, B)
            nc.gpsimd.memset(stack[1][SR:128].bitcast(F32), 0.0).then_inc(tails, 1)
            pool.wait_ge(tails, 3)
            nc.gpsimd.memset(stack[1][SR:SR + 2, 1].bitcast(F32), 1.0).then_inc(tails, 1)
            pool.wait_ge(tails, 4)
            steps = [0]

            def rotate(t, a, half):
                u = t + 2
                n = 512 * half
                for rot, table in ((0, cosT), (1, sinT)):
                    pool.wait_ge(proj_ev, 8 * u + PROJ.index((a, half, rot)) + 1)
                    r = rope[:, rot, n:n + 512]
                    nc.gpsimd.tensor_tensor(r, r, table[:, n:n + 512], ALU.mult).then_inc(rope_step, 1)
                    steps[0] += 1
                pool.wait_ge(rope_step, steps[0])
                nc.gpsimd.tensor_tensor(rope[:, 0, n:n + 512], rope[:, 0, n:n + 512], rope[:, 1, n:n + 512],
                                        ALU.add).then_inc(rope_done, 1)

            def k_low(t, half):
                u = t + 2
                pool.wait_ge(kH_done, 2 * u + HALVES.index(half) + 1)
                n = slice(512 * half, 512 * half + 512)
                nc.gpsimd.tensor_tensor(parts[:, 3, n], rope[:, 0, n], parts[:, 2, n].bitcast(F32),
                                        ALU.subtract).then_inc(kL_done, 1)

            pool.wait_ge(attn_in, 144)
            for t in range(-2, NU):
                for c in range(NC):
                    if t >= 0 and c in DIAG:
                        pool.wait_ge(exp_done, 2 * NC * t + 2 * c + 2)
                        p = probs[:, c % RING, :, 0:128]
                        nc.gpsimd.affine_select(out=p, in_=p, compare_op=ALU.is_ge, fill=0.0, base=0,
                                                pattern=[[0, G], [1, 128]], channel_multiplier=-1).then_inc(sel_done, 1)
                    if t + 2 < NU:
                        if c in ROPE_STEP:
                            rotate(t, *ROPE_STEP[c])
                        if c in KL_STEP:
                            k_low(t, KL_STEP[c])

            for i in range(QD):
                b = i // 2
                q = slice(4 * i, 4 * i + 4)
                pool.wait_ge(z2_done, i + 1)
                nc.gpsimd.tensor_tensor(res[:, q, :], z2[:, q, :], bc[:, 3, b:b + 1, :].to_broadcast([128, 4, C]),
                                        ALU.mult).then_inc(res_step, 1)
                pool.wait_ge(res_step, 2 * i + 1)
                nc.gpsimd.tensor_tensor(res[:, q, :], res[:, q, :], xs[:, q, :], ALU.add).then_inc(res_step, 1)
                pool.wait_ge(res_step, 2 * i + 2)
                nc.gpsimd.tensor_tensor(res[:, q, :], res[:, q, :], bc[:, 4, b:b + 1, :].to_broadcast([128, 4, C]),
                                        ALU.add).then_inc(res_done, 1)

        @block.vector
        def _(dve):
            chain = [0]

            def then(ins):
                chain[0] += 1
                ins.then_inc(dve_step, 1)
                dve.wait_ge(dve_step, chain[0])

            nc.vector.memset(epsc[:], EPS).then_inc(memsets, 1)
            nc.vector.memset(ones[:], 1.0).then_inc(memsets, 1)
            nc.vector.memset(onesb[:], 1.0).then_inc(memsets, 1)
            for p in range(2):
                nc.vector.memset(pm[p][:], NEG).then_inc(memsets, 1)
                then(nc.vector.memset(vu[p][:], 0.0))
                nc.vector.memset(vu[p][:, :, :, HD:HD + 1], 1.0).then_inc(memsets, 1)

            def norm_stats(i, done):
                for n in range(4 * i, 4 * i + 4):
                    ins = nc.vector.bn_stats(bst[:, n, :], xs[:, n, :])
                then(ins)
                for n in range(4 * i, 4 * i + 4):
                    nc.vector.bn_aggr(mv[:, n, :], bst[:, n, :]).then_inc(done, 1)

            def normalise(i, dst, src_std, out_sem):
                dve.wait_ge(src_std, i + 1)
                then(nc.vector.reciprocal(rstd[:, 4 * i:4 * i + 4], std[:, 4 * i:4 * i + 4]))
                for n in range(4 * i, 4 * i + 4):
                    ins = nc.vector.tensor_scalar(dst[:, n, :], xs[:, n, :], mv[:, n, 0:1], rstd[:, n:n + 1],
                                                  ALU.subtract, ALU.mult)
                ins.then_inc(out_sem, 1)

            for i in range(QD):
                dve.wait_ge(x_in[i], 16)
                norm_stats(i, stats)
                if i == 1:
                    dve.wait_ge(silu_e, 1)
                    then(nc.vector.tensor_scalar(sig[:, 2:4], sig[:, 0:2], 1.0, None, ALU.add))
                    then(nc.vector.reciprocal(sig[:, 4:6], sig[:, 2:4]))
                    nc.vector.tensor_tensor(sig[:, 6:8], sig[:, 4:6], cT[:], ALU.mult).then_inc(silu_done, 1)
                if i >= 1:
                    normalise(i - 1, zn, std_done, zn_done)
            dve.wait_ge(qkv_in, 48)
            then(nc.vector.tensor_copy(whi, wraw))
            nc.vector.tensor_copy(wsplit[0:64], wraw[0:64]).then_inc(wsplit_done, 1)
            nc.vector.tensor_tensor(wsplit[64:SR], wraw[64:SR], whi[64:SR].bitcast(F32),
                                    ALU.subtract).then_inc(wsplit_done, 1)
            normalise(QD - 1, zn, std_done, zn_done)
            dve.wait_ge(mod_mm, 1)
            then(nc.vector.tensor_copy(modc[:].rearrange("p k b -> p (k b)"), ps[:, 6, 0:12]))
            nc.vector.tensor_scalar(gate[:, CA, :], modc[:, 1, :], 1.0, None, ALU.add).then_inc(gates_done, 1)
            nc.vector.tensor_copy(gate[:, SA, :], modc[:, 0, :]).then_inc(gates_done, 1)
            nc.vector.tensor_scalar(gate[:, CB, :], modc[:, 4, :], 1.0, None, ALU.add).then_inc(gates_done, 1)
            nc.vector.tensor_copy(gate[:, SBC, :], modc[:, 3, :]).then_inc(gates_done, 1)

            def qk_low(i, a):
                dve.wait_ge(qkH_done, 2 * i + a + 1)
                n = slice(512 * i, 512 * i + 512)
                nc.vector.scalar_tensor_tensor(out=q8[:, 2 * a + 1, n], in0=ps[:, 2 + a, :],
                                               scalar=cols[:, BQ + a:BQ + a + 1], in1=q8[:, 2 * a, n].bitcast(F32),
                                               op0=ALU.add, op1=ALU.subtract).then_inc(qkL_done, 1)

            def v_copy(i):
                dve.wait_ge(v_mm, i + 1)
                nc.vector.tensor_tensor(vnat[:, 4 * i:4 * i + 4, :], ps[:, 4, :].rearrange("p (t c) -> p t c", c=C),
                                        bvb[:].rearrange("p (o c) -> p o c", o=1).to_broadcast([128, 4, C]),
                                        ALU.add).then_inc(v_done, 1)

            for i in range(QD):
                qk_low(i, 0)
                qk_low(i, 1)
                v_copy(i)
            for src, dst in ((2, GA), (5, GB)):
                g = modc[:, src, :]
                then(nc.vector.tensor_scalar(sig[:, 8:10], g, 0.25, None, ALU.max))
                then(nc.vector.scalar_tensor_tensor(out=sig[:, 10:12], in0=g, scalar=-1.0, in1=sig[:, 8:10],
                                                    op0=ALU.mult, op1=ALU.max))
                then(nc.vector.tensor_scalar(sig[:, 12:14], g, 0.0, 2.0, ALU.is_ge, ALU.mult))
                then(nc.vector.scalar_tensor_tensor(out=gate[:, dst, :], in0=sig[:, 12:14], scalar=-1.0,
                                                    in1=sig[:, 10:12], op0=ALU.add, op1=ALU.mult))
            then(nc.vector.tensor_tensor(gate[:, GBC, :], gate[:, GB, :], gate[:, CB, :], ALU.mult))
            then(nc.vector.tensor_tensor(gate[:, GBS, :], gate[:, GB, :], gate[:, SBC, :], ALU.mult))
            then(nc.vector.tensor_scalar(gate[:, GB2, :], gate[:, GB, :], cols[:, B2:B2 + 1], None, ALU.mult))
            dve.wait_ge(m8_mm, 1)
            nc.vector.tensor_tensor(m8[:], ps[:, 5, 0:128], blockd[:], ALU.mult).then_inc(m8_done, 1)
            dve.wait_ge(yb_mm, 1)
            nc.vector.tensor_tensor(yb[:, 0:1], ps[:, 6, 128:129], cols[:, LOB:LOB + 1], ALU.add).then_inc(yb_done, 1)
            dve.wait_ge(yb_mm, 2)
            then(nc.vector.tensor_tensor(yb[:, 1:2], ps[:, 6, 256:257], cols[:, CPB:CPB + 1], ALU.add))
            then(nc.vector.tensor_scalar(gate[:, GAO, :], gate[:, GA, :], yb[:, 1:2], None, ALU.mult))
            dve.wait_ge(const_in, 16)
            for r, which in enumerate(ROWS):
                for b in range(B):
                    ins = nc.vector.tensor_scalar(diag[:, r, b, :], ident[:], gate[:, which, b:b + 1], None, ALU.mult)
            ins.then_inc(diag_done, 1)
            dve.wait_ge(wo_mm, 1)
            dve.wait_ge(bc_done, 3)
            for b in range(B):
                ins = nc.vector.tensor_tensor(woT[:, b, :], ps[:, 4, 0:128], bc[:, 0, b, :], ALU.mult)
            ins.then_inc(wo_done, 1)
            dve.wait_ge(attn_in, 144)
            nc.vector.tensor_copy(identb[:], ident[:]).then_inc(memsets, 1)
            nc.vector.tensor_scalar(maskb[:], tri[:], MASKED, None, ALU.mult).then_inc(memsets, 1)
            then(nc.vector.tensor_scalar(wqk[:], wqk[:], float(L) ** -0.5, None, ALU.mult))
            nc.vector.tensor_scalar(bqk[:], cols[:, WB:WB + 1], float(L) ** -0.5, None, ALU.mult).then_inc(wo_done, 1)

            def q_low(t, ph):
                u, half = t + 2, HALVES[ph]
                dve.wait_ge(qH_done, 2 * u + ph + 1)
                n = slice(512 * half, 512 * half + 512)
                nc.vector.scalar_tensor_tensor(out=parts[:, 1, n], in0=ps[:, work("wqk", ph), :], scalar=bqk[:, 0:1],
                                               in1=parts[:, 0, n].bitcast(F32), op0=ALU.add,
                                               op1=ALU.subtract).then_inc(qL_done, 1)

            def row_max(t, m):
                _, i, part, j, heads = MAXES[m]
                v, w = t + 1, max_width(i, part)
                dve.wait_ge(max_mm, NM * v + m + 1)
                nc.vector.tensor_reduce(pm[v % 2][:, i // 4, i % 4, j:j + heads, part],
                                        ps[:, work("max", m), 0:heads * w].rearrange("p (j n) -> p j n", n=w), AX.X,
                                        ALU.max).then_inc(max_done, 1)

            def row_minima(v, ph):
                half, n = HALVES[ph], 2 * v + ph
                dve.wait_ge(max_done, NM * v + NM_END[ph])
                if n >= 1:
                    dve.wait_ge(nm_tr, n)
                nc.vector.tensor_reduce(nm[:, half], pm[v % 2][:, half], AX.X, ALU.max,
                                        negate=True).then_inc(nm_step, 1)
                dve.wait_ge(nm_step, 2 * n + 1)
                nc.vector.tensor_copy(nms[:, half, :, 0, :], nm[:, half]).then_inc(nm_step, 1)
                dve.wait_ge(nm_step, 2 * n + 2)
                nc.vector.tensor_tensor(nms[:, half, :, 1, :], nm[:, half], nms[:, half, :, 0, :].bitcast(F32),
                                        ALU.subtract).then_inc(nm_done, 1)

            def load_values(v):
                b, g = v // NG, v % NG
                if v >= 2:
                    dve.wait_ge(pv_mm, NC * (v - 1))
                nc.vector.tensor_copy(
                    vu[v % 2][:, :, :, 0:HD],
                    vnat[:, NT * b:NT * b + NT, G * HD * g:G * HD * (g + 1)].rearrange(
                        "p t (j e) -> p t j e", e=HD)).then_inc(vu_done, 1)

            for t in range(-2, NU):
                v = t + 1
                for c in range(NC):
                    if c == LAG + 1 and 0 <= v < NU:
                        load_values(v)
                    for kind, n in STEPS[c]:
                        if kind == "max" and 0 <= v < NU:
                            row_max(t, n)
                            if n + 1 in NM_END:
                                row_minima(v, NM_END.index(n + 1))
                        elif kind == "wqk" and t + 2 < NU:
                            q_low(t, n)

            def part_a(i):
                s = i % 2
                dve.wait_ge(tr1, i + 1)
                o = ps[:, 0:4, :].rearrange("p i (h c) -> p (i h) c", c=32)
                then(nc.vector.reciprocal(recd[:, s, :].rearrange("p (n o) -> p n o", o=1), o[:, :, HD:HD + 1]))
                if i >= 2:
                    dve.wait_ge(tr2, i - 1)
                nc.vector.tensor_tensor(ynat[:, s].rearrange("p t (h e) -> p (t h) e", e=HD), o[:, :, 0:HD],
                                        recd[:, s, :].rearrange("p (n o) -> p n o", o=1).to_broadcast([128, 64, HD]),
                                        ALU.mult).then_inc(ynat_done, 1)
                dve.wait_ge(x1_mm, i + 1)
                dve.wait_ge(xadd_done, B)
                nc.vector.tensor_tensor(xs[:, 4 * i:4 * i + 4, :], ps[:, 5, :].rearrange("p (t c) -> p t c", c=C),
                                        xs[:, 4 * i:4 * i + 4, :], ALU.add).then_inc(x1_done, 1)
                dve.wait_ge(x1_done, i + 1)
                norm_stats(i, stats2)
                normalise(i, z2, std2, z2_done)

            def part_b(i):
                b = i // 2
                dve.wait_ge(f2_mm, i + 1)
                nc.vector.tensor_tensor(proc[:, 4 * i:4 * i + 4, :], ps[:, 5, :].rearrange("p (t c) -> p t c", c=C),
                                        bc[:, 5, b:b + 1, :].to_broadcast([128, 4, C]), ALU.add).then_inc(proc_done, 1)

            def rank(b):
                S = srow[:, T * b:T * b + T]
                S3 = S.rearrange("p (t n) -> p t n", n=128)
                dve.wait_ge(srow_done, 2 * (b + 1))
                if b:
                    dve.wait_ge(rank_mm, b)
                sm = smask.rearrange("p (t n) -> p t n", n=128)
                then(nc.vector.tensor_tensor(sm, S3, ident[:].rearrange("p (o n) -> p o n", o=1).to_broadcast(
                    [128, NT, 128]), ALU.mult))
                nc.vector.tensor_reduce(scol[:, NT * b:NT * b + NT], sm, AX.X, ALU.add).then_inc(scol_done, 1)
                dve.wait_ge(scol_done, b + 1)
                if b:
                    dve.wait_ge(gt_done, 22 * b)
                for j in range(NT):
                    blk = slice(128 * j, 128 * (j + 1))
                    ins = nc.vector.scalar_tensor_tensor(out=eqm[:, blk], in0=S[:, blk], scalar=scol[:, NT * b + j:NT * b + j + 1],
                                                         in1=tri[:], op0=ALU.is_equal, op1=ALU.mult)
                then(ins)
                for j in range(NT):
                    sj = scol[:, NT * b + j:NT * b + j + 1]
                    gj, blk = before[j], slice(128 * j, 128 * (j + 1))
                    if j:
                        nc.vector.tensor_scalar(gj[:, 0:128 * j], S[:, 0:128 * j], sj, None, ALU.is_lt).then_inc(gt_done, 1)
                    if j < NT - 1:
                        nc.vector.tensor_scalar(gj[:, 128 * (j + 1):], S[:, 128 * (j + 1):], sj, None,
                                                ALU.is_le).then_inc(gt_done, 1)
                    nc.vector.scalar_tensor_tensor(out=gj[:, blk], in0=S[:, blk], scalar=sj, in1=eqm[:, blk],
                                                   op0=ALU.is_lt, op1=ALU.add).then_inc(gt_done, 1)

            def finish(b):
                dve.wait_ge(rank_mm, b + 1)
                dve.wait_ge(sig_done, b + 1)
                n = slice(NT * b, NT * b + NT)
                then(nc.vector.scalar_tensor_tensor(out=wsel[:, n], in0=ps[:, 6, 0:NT], scalar=float(KEEP),
                                                    in1=sig[:, n], op0=ALU.is_lt, op1=ALU.mult))
                for t in range(NT * b, NT * b + NT):
                    if t % 4 == 0:
                        dve.wait_ge(proc_done, t // 4 + 1)
                        dve.wait_ge(res_done, t // 4 + 1)
                    nc.vector.scalar_tensor_tensor(out=fin[:, t, :], in0=proc[:, t, :], scalar=wsel[:, t:t + 1],
                                                   in1=res[:, t, :], op0=ALU.mult, op1=ALU.add).then_inc(fin_done, 1)

            part_a(0)
            part_a(1)
            part_b(0)
            part_a(2)
            part_b(1)
            rank(0)
            part_a(3)
            finish(0)
            part_b(2)
            part_b(3)
            rank(1)
            finish(1)


        @block.tensor
        def _(pe):
            mm = nc.tensor.matmul

            def transposes(i):
                pe.wait_ge(zn_done, i + 1)
                if i >= 2:
                    pe.wait_ge(hT_done, i - 1)
                for n in range(4):
                    ins = nc.tensor.transpose(ps[:, i % 2, 128 * n:128 * n + 128], zn[:, 4 * i + n, :], ident[:])
                ins.then_inc(zn_tr, 1)

            pe.wait_ge(const_in, 16)
            transposes(0)
            pe.wait_ge(mod_in, 48)
            pe.wait_ge(silu_done, 1)
            for k in range(6):
                ins = mm(ps[:, 6, B * k:B * k + B], wmod[:, 128 * k:128 * k + 128], sig[:, 6:8], start=True, stop=True)
            ins.then_inc(mod_mm, 1)
            pe.wait_ge(qkv_in, 48)
            for i in range(QD):
                if i + 1 < QD:
                    transposes(i + 1)
                n5 = slice(512 * i, 512 * i + 512)
                pe.wait_ge(hT_done, i + 1)
                for a in range(2):
                    if i:
                        pe.wait_ge(qkL_done, 2 * i - 1 + a)
                    mm(ps[:, 2 + a, :], wqkvT[:, 128 * a:128 * a + 128], hT[:, n5], start=True,
                       stop=True).then_inc(qk_mm, 1)
                if i:
                    pe.wait_ge(v_done, i)
                for n in range(4):
                    ins = mm(ps[:, 4, 128 * n:128 * n + 128], hT[:, 512 * i + 128 * n:512 * i + 128 * n + 128],
                             wqkvT[:, 256:384], start=True, stop=True)
                ins.then_inc(v_mm, 1)
            pe.wait_ge(attn_in, 144)
            mm(ps[:, 5, 0:128], l2oT[:], kvrep[:], start=True, stop=True).then_inc(m8_mm, 1)
            pe.wait_ge(gates_done, 1)
            mm(ps[:, 6, 128:129], l2oT[:], kvb[:], start=True, stop=True).then_inc(yb_mm, 1)
            pe.wait_ge(yb_done, 1)
            mm(ps[:, 6, 256:257], cpT[:], yb[:, 0:1], start=True, stop=True).then_inc(yb_mm, 1)
            pe.wait_ge(m8_done, 1)
            pe.wait_ge(v_done, QD)
            mm(ps[:, 4, 0:128], m8[:], cpT[:], start=True, stop=True).then_inc(wo_mm, 1)
            pe.wait_ge(memsets, 2)
            pe.wait_ge(diag_done, 1)
            flat = diag.rearrange("p r b c -> p (r b c)")
            for n in range(3):
                mm(ps[:, 5 + n, :], ones[:], flat[:, 512 * n:512 * n + 512], start=True, stop=True).then_inc(bc_mm, 1)
            pe.wait_ge(bc_done, 3)
            pe.wait_ge(wo_done, 2)
            pe.wait_ge(wsplit_done, 2)
            pe.wait_ge(memsets, 8)

            last = {4: None, 5: None, 7: None}

            def bank_free(kind, n, u):
                bank = work(kind, n)
                if last[bank]:
                    before_kind, m, v = last[bank]
                    if before_kind == "proj":
                        pe.wait_ge(proj_ev, 8 * v + m + 1)
                    elif before_kind == "wqk":
                        pe.wait_ge(qH_done, 2 * v + m + 1)
                        pe.wait_ge(qL_done, 2 * v + m + 1)
                    elif before_kind == "turn":
                        pe.wait_ge(nmT_done, 2 * v + m + 1)
                    else:
                        pe.wait_ge(max_done, NM * v + m + 1)
                last[bank] = (kind, n, u)
                return ps[:, bank, :]

            def project(t, n):
                a, half, rot = PROJ[n]
                u = t + 2
                if n == 0:
                    pe.wait_ge(s8_in, 48 * (u + 1))
                mm(bank_free("proj", n, u), wsplit[:, 2 * a + rot, :], s8[:, a, 512 * half:512 * half + 512], start=True,
                   stop=True).then_inc(proj_mm, 1)

            def map_q(t, ph):
                u, half = t + 2, HALVES[ph]
                pe.wait_ge(rope_done, 4 * u + ph + 1)
                mm(bank_free("wqk", ph, u), wqk[:], rope[:, 0, 512 * half:512 * half + 512], start=True, stop=True).then_inc(wqk_mm, 1)

            def max_scores(t, m):
                ph, i, part, j0, heads = MAXES[m]
                v, w = t + 1, max_width(i, part)
                st = stack[v % 2]
                k0 = 512 * part
                diagonal = k0 + w == 128 * (i + 1)
                if m == 0:
                    pe.wait_ge(half_in[1], 96 * (v + 1))
                if part == 0:
                    pe.wait_ge(half_in[0], 96 * (v + 1))
                bank = bank_free("max", m, v)[:, 0:heads * w].rearrange("p (j n) -> p j n", n=w)
                for j in range(heads):
                    ins = mm(bank[:, j, :], st[0:SR, 0, j0 + j, 128 * i:128 * i + 128], st[0:SR, 1, j0 + j, k0:k0 + w],
                             start=True, stop=not diagonal, skip_group_check=True)
                if diagonal:
                    ins = mm(bank[:, :, w - 128:w], identb[:],
                             maskb[:].rearrange("p (o n) -> p o n", o=1).to_broadcast([128, heads, 128]),
                             start=False, stop=True, skip_group_check=True)
                ins.then_inc(max_mm, 1)

            def turn(v, ph):
                pe.wait_ge(nm_done, 2 * v + ph + 1)
                bank = bank_free("turn", ph, v)
                for i in range(4):
                    ins = nc.tensor.transpose(bank[0:2 * G, 128 * i:128 * i + 128],
                                              nms[:, HALVES[ph], i].bitcast(F32).rearrange("p s j -> p (s j)"), ident[:])
                ins.then_inc(nm_tr, 1)

            def scores(t, c, pair):
                _, q, k, off, w = CHUNKS[c]
                st = stack[t % 2]
                if NC * t + c >= 1:
                    pe.wait_ge(exp_done, 2 * NC * t + 2 * (c - 1) + pair + 1)
                for n in range(2):
                    j = 2 * pair + n
                    ins = mm(E[pair][:, n, 0:w], st[:, 1, j, 128 * k:128 * k + 128],
                             st[:, 0, j, 512 * q + off:512 * q + 512], start=True, stop=True)
                ins.then_inc(score_mm, 1)

            def values(t, c):
                ph, q, k, off, w = CHUNKS[c]
                if c in DIAG:
                    pe.wait_ge(sel_done, len(DIAG) * t + DIAG.index(c) + 1)
                else:
                    pe.wait_ge(exp_done, 2 * NC * t + 2 * c + 2)
                if k == 0 and 2 * t + ph > 0:
                    pe.wait_ge(o_done, 2 * t + ph)
                for j in range(G):
                    ins = mm(O[32 * j:32 * j + 32, off:512], vu[t % 2][:, k, j, :], probs[:, c % RING, j, 0:w],
                             start=(k == 0), stop=(c in LAST), skip_group_check=True)
                ins.then_inc(pv_mm, 1)

            for t in range(-2, NU):
                for c in range(NC):
                    if c in (0, LAST[0] + 1) and t >= 0:
                        pe.wait_ge(row_in[HALVES[CHUNKS[c][0]]], 32 * (t + 1))
                    if c == 0 and t >= 0:
                        pe.wait_ge(tails, min(2 * t + 2, 4))
                        pe.wait_ge(vu_done, t + 1)
                    for kind, n in STEPS[c]:
                        if kind == "scores" and t >= 0:
                            scores(t, c, n)
                        elif kind == "values" and c >= LAG and t >= 0:
                            values(t, c - LAG)
                        elif kind == "values" and c < LAG and t >= 1:
                            values(t - 1, NC + c - LAG)
                        elif kind == "max" and 0 <= t + 1 < NU:
                            max_scores(t, n)
                        elif kind == "proj" and t + 2 < NU:
                            project(t, n)
                        elif kind == "wqk" and t + 2 < NU:
                            map_q(t, n)
                        elif kind == "turn" and 0 <= t + 1 < NU:
                            turn(t + 1, n)
            for c in range(NC - LAG, NC):
                values(NU - 1, c)

            def part_a(i, f1s, f2s):
                b, s = i // 2, i % 2
                if i == 0:
                    pe.wait_ge(o_done, 2 * NU)
                if f1s:
                    pe.wait_ge(gelu_done, FT * f1s)
                for n in range(4):
                    for g in range(NG):
                        n0 = 512 * (i % 2) + 128 * n
                        ins = nc.tensor.transpose(ps[:, n, 128 * g:128 * g + 128], oT[:, NG * b + g, n0:n0 + 128],
                                                  ident[:])
                ins.then_inc(tr1, 1)
                pe.wait_ge(ynat_done, i + 1)
                if i:
                    pe.wait_ge(yT_done, i)
                for n in range(4):
                    ins = nc.tensor.transpose(ps[:, 4, 128 * n:128 * n + 128], ynat[:, s, n, :], ident[:])
                ins.then_inc(tr2, 1)
                pe.wait_ge(yT_done, i + 1)
                if i:
                    pe.wait_ge(x1_done, i)
                if f2s:
                    pe.wait_ge(proc_done, f2s)
                for n in range(4):
                    ins = mm(ps[:, 5, 128 * n:128 * n + 128], yT[:, s, 128 * n:128 * n + 128], woT[:, b, :],
                             start=True, stop=True)
                ins.then_inc(x1_mm, 1)

            def part_b(i, tr1s):
                b, s = i // 2, i % 2
                pe.wait_ge(z2_done, i + 1)
                if i:
                    pe.wait_ge(h2T_done, i)
                if i == 2:
                    pe.wait_ge(fin_done, 1)
                for n in range(4):
                    ins = nc.tensor.transpose(ps[:, 6, 128 * n:128 * n + 128], z2[:, 4 * i + n, :], ident[:])
                ins.then_inc(tr3, 1)
                n5 = slice(512 * i, 512 * i + 512)
                pe.wait_ge(h2T_done, i + 1)
                if i:
                    pe.wait_ge(srow_done, i)
                pe.wait_ge(ffn_in, 64)
                mm(ps[:, 7, :], wrb[:], h2T[:, n5], start=True, stop=True).then_inc(sc_mm, 1)
                pe.wait_ge(ynat_done, tr1s)
                for f in range(FT):
                    if i:
                        pe.wait_ge(gelu_done, FT * (i - 1) + f + 1)
                    mm(ps[:, f, :], w1[:, 128 * f:128 * f + 128], h2T[:, n5], start=True,
                       stop=True).then_inc(f1_mm, 1)
                pe.wait_ge(gelu_done, FT * (i + 1))
                pe.wait_ge(w2g_done, B)
                pe.wait_ge(x1_done, tr1s)
                if i:
                    pe.wait_ge(proc_done, i)
                for n in range(4):
                    for f in range(FT):
                        ins = mm(ps[:, 5, 128 * n:128 * n + 128], actT[:, s, f, 128 * n:128 * n + 128],
                                 w2g[:, b, f, :], start=(f == 0), stop=(f == FT - 1))
                ins.then_inc(f2_mm, 1)

            def rank(b):
                pe.wait_ge(gt_done, 22 * (b + 1))
                pe.wait_ge(h2T_done, 2 * (b + 1))
                for i in range(NT):
                    for j in range(NT):
                        ins = mm(ps[:, 6, i:i + 1], before[j][:, 128 * i:128 * i + 128], onesb[:, 0:1],
                                 start=(j == 0), stop=(j == NT - 1))
                ins.then_inc(rank_mm, 1)

            part_a(0, 0, 0)
            part_a(1, 0, 0)
            part_b(0, 2)
            part_a(2, 1, 1)
            part_b(1, 3)
            part_a(3, 2, 2)
            rank(0)
            part_b(2, 4)
            part_b(3, 4)
            rank(1)


def lay_out(i):
    f = {k: np.asarray(v) for k, v in i.items()}
    cols = np.zeros((128, 16), np.float32)
    wc, bcn = f["L0_attn_c_attn_w"], f["L0_attn_c_attn_b"]
    swap = np.arange(L) ^ 1
    cols[:, 0], cols[:, 1] = bcn[0:C], bcn[C:2 * C]
    cols[:, 2] = np.repeat(f["L0_attn_q2l_b"], G)
    cols[:, 3] = np.repeat(f["L0_attn_q2l_b"][swap], G)
    cols[:, 4] = np.repeat(f["L0_attn_kv2l_b"], G)
    cols[:, 5] = np.repeat(f["L0_attn_kv2l_b"][swap], G)
    cols[:, 6] = np.repeat(f["L0_attn_wqk_b"], G)
    cols[:, 7] = np.tile(f["L0_attn_l2o_b"], H)
    cols[:, 8] = f["L0_attn_cproj_b"]
    cols[:, 9] = f["L0_ffn_b2"]
    cols[:, 10:10 + FT] = f["L0_ffn_b1"].reshape(FT, 128).T
    wlat = np.zeros((3, G, HD, 4, L, G), np.float32)
    wqk = np.zeros((L, G, L, G), np.float32)
    for j in range(G):
        for k, w in enumerate((f["L0_attn_q2l_w"], f["L0_attn_q2l_w"][swap],
                               f["L0_attn_kv2l_w"], f["L0_attn_kv2l_w"][swap])):
            wlat[:, j, :, k, :, j] = w.T
        wqk[:, j, :, j] = f["L0_attn_wqk_w"].T
    inv = (np.float32(1.0) / np.float32(10000.0) ** (np.arange(0, L, 2, dtype=np.float32) / np.float32(L)))
    ang = np.repeat(np.outer(np.arange(T, dtype=np.float32), inv.astype(np.float32)), 2, axis=1).astype(np.float32)
    sign = np.where(np.arange(L) % 2 == 0, -1.0, 1.0)
    cos = np.repeat(np.cos(ang.astype(np.float64)).T, G, axis=0).astype(np.float32)
    sin = np.repeat((np.sin(ang.astype(np.float64)) * sign).T, G, axis=0).astype(np.float32)
    at = np.arange(128)
    return {
        "x": f["L0_attn_x"], "ident": np.eye(128, dtype=np.float32),
        "tri": (at[None, :] > at[:, None]).astype(np.float32),
        "blockd": (at[None, :] // HD == at[:, None] // HD).astype(np.float32),
        "cos": cos, "sin": sin, "cT": f["L0_c"].T,
        "wmod": f["L0_wmod"], "cols": cols,
        "wqkvT": wc.T, "bv": np.broadcast_to(bcn[2 * C:], (128, C)), "wlat": wlat.reshape(SR, 4, 128),
        "wqk": wqk.reshape(128, 128), "cpT": f["L0_attn_cproj_w"].T,
        "l2oT": np.tile(f["L0_attn_l2o_w"].T, (1, H)), "kvrep": np.tile(f["L0_attn_kv2l_w"], (1, H)),
        "kvb": f["L0_attn_kv2l_b"].reshape(L, 1), "w1": f["L0_ffn_W1"],
        "w2": f["L0_ffn_W2"].reshape(FT, 128, C).transpose(1, 0, 2),
        "wr": np.broadcast_to(f["L0_ffn_w_router"][:, None], (C, 128)),
    }


def kernel(**inputs):
    import concourse.bacc as bacc
    from concourse.bass_utils import run_bass_kernel_spmd

    nc = bacc.Bacc("TRN2", target_bir_lowering=False, num_devices=1)
    arrays, d = {}, {}
    for name, a in lay_out(inputs).items():
        a = np.ascontiguousarray(a)
        arrays[f"in_{name}"] = a
        d[name] = nc.dram_tensor(f"in_{name}", a.shape, mybir.dt.from_np(a.dtype), kind="ExternalInput").ap()
    out = nc.dram_tensor("out_x", (B, T, C), F32, kind="ExternalOutput").ap()
    adaln_block(nc, d, out)
    r = run_bass_kernel_spmd(nc, [arrays], core_ids=[0])
    return r.results[0]["out_x"]
```

```python
from contextlib import ExitStack

import numpy as np
import concourse.bass as bass
from concourse import mybir

F32 = mybir.dt.float32
F32R = mybir.dt.float32r
BF16 = mybir.dt.bfloat16
ACT = mybir.ActivationFunctionType
ALU = mybir.AluOpType
AX = mybir.AxisListType

B, T, C = 2, 1024, 128
H, HD, L = 16, 8, 32
F = 512
KEEP = T // 2
G = 4
NG = H // G
NU = B * NG
NT = T // 128
QD = B * T // 512
FT = F // 128
COMPARES = 3 * NT - 2
SR = 3 * L
NEG = -3.0e38
MASKED = -1.0e30
EPS = 1e-5

HALVES = [1, 0]
CHUNKS = [(ph, q, k, max(0, 128 * k - 512 * q), 512 - max(0, 128 * k - 512 * q))
          for ph, q in enumerate(HALVES) for k in range(4 * (q + 1))]
NC = len(CHUNKS)
DIAG = [n for n, (_, q, k, _, _) in enumerate(CHUNKS) if 128 * k >= 512 * q]
LAST = [max(n for n in range(NC) if CHUNKS[n][0] == ph) for ph in range(2)]


def max_width(i, part):
    return min(512, 128 * (i + 1) - 512 * part)


MAXES = [(ph, i, part, j, max(1, min(G, 512 // max_width(i, part))))
         for ph, q in enumerate(HALVES) for part in range(q, -1, -1) for i in range(4 * q, 4 * q + 4)
         for j in range(0, G, max(1, min(G, 512 // max_width(i, part))))]
NM = len(MAXES)
RING = 3
LAG = 2
FIRST_MAX = 1

ORDER = [0, 1, 3, 2]
LATE = {(NU - 2, 6): [("yT", 0)], (NU - 2, 7): [("x1", 0), ("yT", 1)], (NU - 2, 8): [("x1", 1), ("z", 0)],
        (NU - 2, 9): [("z", 1)],
        (NU - 1, 0): [("zT", 0)], (NU - 1, 1): [("zT", 1), ("router", 0)], (NU - 1, 2): [("router", 1)],
        (NU - 1, 3): [("compare", 0)], (NU - 1, 4): [("f1", 0), ("gelu", 0), ("f1", 1), ("gelu", 1)],
        (NU - 1, 6): [("f2", 0)], (NU - 1, 8): [("f2", 1)], (NU - 1, 11): [("weights", 0)]}
TAIL = [("yT", 2), ("norm", 1), ("x1", 2), ("rank", 0), ("yT", 3), ("z", 2), ("x1", 3), ("z", 3),
        ("zT", 2), ("router", 2), ("zT", 3), ("fin", 0), ("fin", 1), ("router", 3), ("f1", 2), ("compare", 1),
        ("gelu", 2), ("f1", 3), ("f2", 2), ("gelu", 3), ("weights", 1), ("f2", 3), ("rank", 1), ("fin", 2),
        ("fin", 3)]
LATE_BANK = {"yT": (4,) * 4, "x1": (5,) * 4, "zT": (7,) * 4, "router": (4,) * 4,
             "compare": (7,) * 2, "rank": (5,) * 2, "f2": (5, 7, 6, 7)}
F1_BANK = ((4, 5, 7, 4), (5, 7, 4, 5), (0, 1, 2, 3), (0, 1, 2, 3))
MAPS_AT = 2
ROWS_AT = 5
PROJ = [(a, half, rot) for a in range(2) for half in HALVES for rot in range(2)]
JOBS = {(0, 0): ("proj", 0), (0, 1): ("proj", 1), (1, 0): ("proj", 2), (1, 1): ("proj", 3),
        (2, 0): ("wqk", 0), (2, 1): ("proj", 4), (3, 0): ("proj", 5), (4, 0): ("wqk", 1),
        (4, 1): ("proj", 6), (5, 0): ("proj", 7),
        (3, 1): ("norm", 1), (11, 0): ("norm", 0)}
ROPE_STEP = {1: (0, 1), 2: (0, 0), 3: (1, 1), 5: (1, 0)}
KH_STEP = {5: 1, 7: 0}
KL_STEP = {6: 1, 8: 0}


STEP_COST, COPY_COST, HIGH_COST, JOB_COST, LATE_COST, BEFORE_COST, MAX_COST = 400, 600, 600, 650, 800, 2000, 90


def plan(t):
    prep, first = t + 2 < NU, FIRST_MAX if t >= 0 else 0
    act = [(G * w + STEP_COST + COPY_COST * (c in COPY_STEP) if t >= 0 else BEFORE_COST) +
           HIGH_COST * (c in KH_STEP and prep) +
           JOB_COST * sum(JOBS.get((c, p), ("norm", 0))[0] != "norm" and prep for p in range(2)) +
           LATE_COST * len(LATE.get((t, c), ())) for c, (_, _, _, _, w) in enumerate(CHUNKS)]
    cost = [max_width(i, part) * n + MAX_COST for _, i, part, _, n in MAXES]
    steps, m, at, phases = [], 0, 0, 0
    for c in range(NC):
        mine = []
        while m < NM and c >= first and at + cost[m] / 2 < sum(cost) * sum(act[first:c + 1]) / sum(act[first:]):
            at += cost[m]
            mine.append(("max", m))
            m += 1
        order = []
        for left, rest in ((4, [("scores", 0)]), (3, [JOBS.get((c, 0)), ("scores", 1)]),
                           (2, [("values", 0)]), (1, [JOBS.get((c, 1))])):
            share = -(-len(mine) // left)
            order += mine[:share] + [x for x in rest if x]
            mine = mine[share:]
        if phases < 2 and (c == NC - 1 or m > NM_END[phases]):
            order.append(("turn", phases))
            phases += 1
        steps.append(order)
    return steps


COPY_STEP = [(LAST[ph] + LAG + 1) % NC for ph in range(2)]
NM_END = [max(m for m in range(NM) if MAXES[m][0] == ph) + 1 for ph in range(2)]
STEPS = {t: plan(t) for t in range(-1, NU)}
BANKED = {t: [x for order in STEPS[t] for x in order if x[0] not in ("scores", "values")] for t in STEPS}


def adaln_block(nc, d, out):
    with ExitStack() as ctx:
        def sb(name, shape, dt=F32):
            return ctx.enter_context(nc.sbuf_tensor(name, shape, dt))

        def sem(name):
            return ctx.enter_context(nc.semaphore(name))

        xs = sb("xs", [128, B * NT, C])
        consts = sb("consts", [128, 272])
        ident = consts[:, 0:128]
        bvb = consts[:, 128:256]
        cols = consts[:, 256:272]
        weights = sb("weights", [128, 1024])
        wqk, cpT = weights[:, 0:128], weights[:, 128:256]
        tri = weights[:, 256:384]
        wrb = weights[:, 384:512]
        w1 = weights[:, 512:1024]
        tables = sb("tables", [128, 2 * T])
        cosT, sinT = tables[:, 0:T], tables[:, T:2 * T]
        identb = sb("identb", [128, 128], BF16)
        maskb = sb("maskb", [128, 128], BF16)
        ones = sb("ones", [128, 128])
        wsplit = sb("wsplit", [SR, 4, 128], F32R)
        bqk = sb("bqk", [128, 1])
        w2g = sb("w2g", [128, B, FT, C])
        woT = sb("woT", [128, B, C])
        bc = sb("bc", [128, 6, B, C])
        modc = sb("modc", [128, 6, B])
        gate = sb("gate", [128, 10, B])
        yb = sb("yb", [128, 4])
        vnat = sb("vnat", [128, B * NT, C])
        vu = [sb(f"vu{p}", [128, NT, G, 32]) for p in range(2)]
        parts = sb("parts", [128, 4, T], F32R)
        rope = sb("rope", [128, 2, T])
        s8 = sb("s8", [SR, 2, T], F32R)
        probs = sb("probs", [128, RING, G, 512])
        oc = sb("oc", [128, 2, 512])
        ynat = sb("ynat", [128, B * NT, C])
        extra = sb("extra", [128, 5120])
        pm = [sb(f"pm{p}", [128, 2, 4, G, 2]) for p in range(2)]
        nm = sb("nm", [128, 2, G, 4])
        nms = sb("nms", [128, 2, G, 2, 4], F32R)
        nmT_both = sb("nmT", [64, 128])
        nmT = [nmT_both[0:8 * G], nmT_both[32:32 + 8 * G]]
        bst = sb("bst", [128, B * NT, 6])
        mv = sb("mv", [128, B * NT, 2])
        std = sb("std", [128, B * NT])
        rstd = sb("rstd", [128, B * NT])
        epsc = sb("epsc", [128, 1])
        onesb = sb("onesb", [128, 2], BF16)
        scol = sb("scol", [128, B * NT])
        wsel = sb("wsel", [128, B * NT])
        sig = sb("sig", [128, B * NT])
        recd = sb("recd", [128, 2, 4 * G])

        with ExitStack() as shared:
            stack = [shared.enter_context(nc.sbuf_tensor(f"stack{p}", [128, 2, G, T], F32R))
                     for p in range(2)]
        late, late2 = sb("late", [128, 2 * G * T]), sb("late2", [128, 2 * G * T])

        early = probs[:].rearrange("p r j n -> p (r j n)")
        hT = early[:, 0:2048]
        zn = early[:, 2048:4096].rearrange("p (t c) -> p t c", c=C)
        cT, wmod = extra[:, 0:2], extra[:, 2:770]
        wqkvT, blockd = extra[:, 770:1154], extra[:, 1154:1282]
        diag = extra[:, 1282:2818].rearrange("p (r b c) -> p r b c", r=6, b=B)
        wraw = extra[0:SR, 2818:3330].rearrange("p (k m) -> p k m", k=4)
        m8 = extra[:, 3330:3458]
        l2oT, kvrep, kvb = extra[0:L, 3458:3586], extra[0:L, 3586:3714], extra[0:L, 3714:3715]
        whi = parts[0:SR, 0, 0:512].rearrange("p (k m) -> p k m", k=4)
        q8 = stack[1][:].rearrange("p a j t -> p (a j t)").rearrange("p (k n) -> p k n", k=4)
        z2 = extra[:, 0:2048].rearrange("p (t c) -> p t c", c=C)
        res = extra[:, 2048:4096].rearrange("p (t c) -> p t c", c=C)
        yT = extra[:, 4096:5120].rearrange("p (s n) -> p s n", s=2)
        h2T, srow = late[:, 0:2048], late[:, 2048:4096]
        eqm = late[:, 5120:6144]
        proc = late[:, 6144:8192].rearrange("p (t c) -> p t c", c=C)
        actT = parts[:].bitcast(F32).rearrange("p k n -> p (k n)").rearrange("p (s f n) -> p s f n", s=2, f=FT)
        fin = late2[:, 4096:6144].rearrange("p (t c) -> p t c", c=C)
        before = [rope[:, n // 2, :].bitcast(BF16)[:, T * (n % 2):T * (n % 2) + T] for n in range(4)] + \
                 [tables[:].bitcast(BF16)[:, T * n:T * n + T] for n in range(4)]

        ps = ctx.enter_context(nc.psum_tensor("ps", [128, 8, 512], F32))
        E = [ps[:, 0:2, :], ps[:, 2:4, :]]
        O = ps[:, 6, :]

        def work(t, kind, n):
            banks = (4, 5, 7) if t >= 0 else (4, 5, 7, 3)
            return banks[BANKED[t].index((kind, n)) % len(banks)]

        FIRST = [("proj", 0), ("proj", 1), ("proj", 4), ("proj", 5), ("wqk", 0), ("proj", 2), ("proj", 3), ("wqk", 1),
                 ("proj", 6), ("proj", 7)]
        first_proj = [n for kind, n in FIRST if kind == "proj"]

        def prep_bank(u, kind, n):
            return (5, 6, 7, 0, 1, 2, 3, 4, 5, 6)[FIRST.index((kind, n))] if u == 0 else work(u - 2, kind, n)

        def proj_count(u, n):
            return 8 * u + (first_proj.index(n) if u == 0 else n) + 1

        def rope_count(u, a, half):
            ph = HALVES.index(half)
            return 4 * u + (2 * ph + a if u == 0 else 2 * a + ph) + 1

        def rope_at(u, a, half):
            n = 512 * (1 - a if u == 0 else half)
            return slice(n, n + 512)

        x_in = [sem(f"x_in{i}") for i in range(QD)]
        mod_in, qkv_in, attn_in, ffn_in, const_in = (sem(n) for n in (
            "mod_in", "qkv_in", "attn_in", "ffn_in", "const_in"))
        memsets = sem("memsets")
        silu_e, silu_done, mod_mm = (sem(n) for n in ("silu_e", "silu_done", "mod_mm"))
        gates_done, gao_done, diag_done, bc_mm, bc_done = (sem(n) for n in (
            "gates_done", "gao_done", "diag_done", "bc_mm", "bc_done"))
        m8_mm, m8_done, yb_mm, yb_done, wo_mm, wo_done = (sem(n) for n in (
            "m8_mm", "m8_done", "yb_mm", "yb_done", "wo_mm", "wo_done"))
        dve_step = sem("dve_step")
        stats, std_done, zn_done, zn_tr, hT_done = (sem(n) for n in (
            "stats", "std_done", "zn_done", "zn_tr", "hT_done"))
        qk_mm, qkH_done, qkL_done, v_mm, v_done = (sem(n) for n in (
            "qk_mm", "qkH_done", "qkL_done", "v_mm", "v_done"))
        wsplit_done, xadd_done, w2g_done = (sem(n) for n in ("wsplit_done", "xadd_done", "w2g_done"))
        q8_out, s8_in = [sem(f"q8_out{b}") for b in range(B)], sem("s8_in")
        proj_mm, proj_ev, rope_done, rope_step = (sem(n) for n in ("proj_mm", "proj_ev", "rope_done", "rope_step"))
        wqk_mm, qH_done, qL_done, kH_done, kL_done = (sem(n) for n in (
            "wqk_mm", "qH_done", "qL_done", "kH_done", "kL_done"))
        half_in = [sem(f"half_in{h}") for h in range(2)]
        row_in, vu_done = [sem(f"row_in{h}") for h in range(2)], sem("vu_done")
        tails, tails_in = sem("tails"), sem("tails_in")
        max_mm, max_done, nm_step, nm_done, nm_tr, nmT_done = (sem(n) for n in (
            "max_mm", "max_done", "nm_step", "nm_done", "nm_tr", "nmT_done"))
        score_mm, exp_done, sel_done, pv_mm, o_done = (sem(n) for n in (
            "score_mm", "exp_done", "sel_done", "pv_mm", "o_done"))
        o_tr, ynat_done, yT_mm, yT_done, x1_mm, x1_done = (sem(n) for n in (
            "o_tr", "ynat_done", "yT_mm", "yT_done", "x1_mm", "x1_done"))
        stats2, std2, z2_done, zT_mm, h2T_done, sc_mm, srow_done = (sem(n) for n in (
            "stats2", "std2", "z2_done", "zT_mm", "h2T_done", "sc_mm", "srow_done"))
        f1_mm, gelu_done, f2_mm, proc_done, res_step, res_done = (sem(n) for n in (
            "f1_mm", "gelu_done", "f2_mm", "proc_done", "res_step", "res_done"))
        scol_mm = sem("scol_mm")
        scol_done, gt_done, rank_mm, sig_done, wsel_done, fin_done, out_done = (sem(n) for n in (
            "scol_done", "gt_done", "rank_mm", "sig_done", "wsel_done", "fin_done", "out_done"))

        scratch = nc.dram_tensor("q8_scratch", [128, 4, B * T], F32, kind="Internal").ap()

        block = ctx.enter_context(nc.Block())

        CA, SA, CB, SBC, GA, GAO, GB, GBC, GBS, GB2 = range(10)
        ROWS = [GA, GAO, GB, GBC, GBS, GB2]
        BQ, BK, QB, QRB, KB, KRB, WB, LOB, CPB, B2 = range(10)
        B1 = 10

        @block.sync
        def _(sp):
            xd = d["x"].rearrange("b (t p) c -> p (b t) c", p=128)
            for i in range(QD):
                sp.dma_start(xs[:, 4 * i:4 * i + 4, :], xd[:, 4 * i:4 * i + 4, :]).then_inc(x_in[i], 16)
                if i == 0:
                    sp.dma_start(consts[:], d["consts"]).then_inc(const_in, 16)
            sp.dma_start(tables[:], d["tables"]).then_inc(attn_in, 16)
            for b in range(B):
                sp.dma_start(w2g[:, b], d["w2"]).then_inc(ffn_in, 16)

            def load_s8(u):
                b, g = (u // NG, u % NG)
                for s, part in enumerate((0, 1, 0)):
                    src = scratch[g * 32:(g + 1) * 32, part::2, b * T:(b + 1) * T]
                    if u == 0:
                        src = q8[0:32, part::2, 0:T].bitcast(F32)
                    sp.dma_start(s8[s * 32:(s + 1) * 32, :, :].bitcast(F32), src).then_inc(s8_in, 16)

            for b in range(B):
                sp.wait_ge(qkH_done, 4 * (b + 1))
                sp.wait_ge(qkL_done, 4 * (b + 1))
                if b == 0:
                    load_s8(0)
                sp.dma_start(scratch[:, :, b * T:(b + 1) * T],
                             q8[:, :, b * T:(b + 1) * T].bitcast(F32)).then_inc(q8_out[b], 16)

            def load_half(u, half):
                n, ph = slice(512 * half, 512 * half + 512), HALVES.index(half)
                for done in (qH_done, qL_done, kH_done, kL_done):
                    sp.wait_ge(done, 2 * u + ph + 1)
                if u >= 2:
                    sp.wait_ge(score_mm, 2 * (NC * (u - 2) + LAST[ph] + 1))
                for a, rows in ((0, (0, 1, 0)), (1, (2, 2, 3))):
                    for s, part in enumerate(rows):
                        sp.dma_start(stack[u % 2][s * 32:(s + 1) * 32, a, :, n].bitcast(F32),
                                     parts[:, part, n].bitcast(F32)).then_inc(half_in[half], 16)

            def load_rows(u, half):
                sp.wait_ge(nmT_done, 2 * u + HALVES.index(half) + 1)
                if u == 0:
                    sp.wait_ge(tails_in, 16)
                for j in range(G):
                    row = stack[u % 2][SR:SR + 2, 0, j, 512 * half:512 * half + 512].bitcast(F32)
                    sp.dma_start(row, nmT[half][8 * j:8 * (j + 1), :]).then_inc(row_in[half], 16)

            for t in range(-2, NU):
                if t == -2:
                    load_half(0, HALVES[0])
                    sp.wait_ge(q8_out[0], 16)
                if t + 3 < NU:
                    sp.wait_ge(proj_mm, 8 * (t + 3))
                    load_s8(t + 3)
                for half in HALVES:
                    if 0 <= t + 1 < NU:
                        load_rows(t + 1, half)
                    if t + 2 < NU and (t > -2 or half != HALVES[0]):
                        load_half(t + 2, half)
                if t == -2:
                    sp.wait_ge(s8_in, 96)
                    sp.wait_ge(q8_out[1], 16)
                    sp.wait_ge(tails, 2)
                    sp.dma_start(stack[1][SR:128].bitcast(F32), stack[0][SR:128].bitcast(F32)).then_inc(tails_in, 16)
            od = out.rearrange("b (t p) c -> p (b t) c", p=128)
            for k, i in enumerate(ORDER):
                sp.wait_ge(fin_done, 4 * (k + 1))
                sp.dma_start(od[:, 4 * i:4 * i + 4, :], fin[:, 4 * i:4 * i + 4, :]).then_inc(out_done, 16)
            sp.wait_ge(out_done, 16 * QD)

        @block.scalar
        def _(act):
            act.dma_start(extra[:, 0:770], d["mod"]).then_inc(mod_in, 16)
            act.dma_start(extra[:, 770:1282], d["qkv"]).then_inc(qkv_in, 16)
            act.dma_start(wraw, d["wlat"]).then_inc(attn_in, 16)
            act.dma_start(weights[:], d["weights"]).then_inc(attn_in, 16)
            act.dma_start(extra[0:L, 3458:3715], d["vmap"]).then_inc(attn_in, 16)
            act.wait_ge(mod_in, 16)
            nc.scalar.activation(sig[:, 0:B], cT, ACT.Exp, scale=-1.0).then_inc(silu_e, 1)
            act.wait_ge(memsets, 1)

            def deviation(i):
                act.wait_ge(stats, 4 * (i + 1))
                nc.scalar.activation(std[:, 4 * i:4 * i + 4], mv[:, 4 * i:4 * i + 4, 1], ACT.Sqrt,
                                     bias=epsc[:, 0:1]).then_inc(std_done, 1)

            deviation(0)
            deviation(1)

            def qk_high(i, a):
                act.wait_ge(qk_mm, 2 * i + a + 1)
                nc.scalar.activation(q8[:, 2 * a, 512 * i:512 * i + 512], ps[:, 2 + a, :], ACT.Identity,
                                     bias=cols[:, BQ + a:BQ + a + 1]).then_inc(qkH_done, 1)

            act.wait_ge(gates_done, 4)
            act.wait_ge(const_in, 16)
            for i in range(QD):
                b = i // 2
                act.wait_ge(zn_tr, i + 1)
                nc.scalar.activation(hT[:, 512 * i:512 * i + 512], ps[:, i % 2, :], ACT.Identity,
                                     bias=gate[:, SA, b:b + 1], scale=gate[:, CA, b:b + 1]).then_inc(hT_done, 1)
                if i + 2 < QD:
                    deviation(i + 2)
                if i:
                    qk_high(i - 1, 0)
                    qk_high(i - 1, 1)
            qk_high(QD - 1, 0)
            qk_high(QD - 1, 1)

            def projected(t, n):
                a, half, rot = PROJ[n]
                u, ph = t + 2, HALVES.index(half)
                act.wait_ge(proj_mm, proj_count(u, n))
                if u == 0 and n in (2, 3):
                    act.wait_ge(wqk_mm, 1)
                if u == 0 and n in (6, 7):
                    act.wait_ge(kH_done, 1)
                    act.wait_ge(kL_done, 1)
                if a == 0 and u > 0:
                    last_k = 2 if u == 1 else 2 * u - 1 + ph
                    act.wait_ge(kH_done, last_k)
                    act.wait_ge(kL_done, last_k)
                if a == 1 and u > 0:
                    act.wait_ge(wqk_mm, 2 * u + ph + 1)
                bias = cols[:, QB + 2 * a + rot:QB + 2 * a + rot + 1]
                nc.scalar.activation(rope[:, rot, rope_at(u, a, half)], ps[:, prep_bank(u, "proj", n), :], ACT.Identity,
                                     bias=bias).then_inc(proj_ev, 1)

            def q_high(t, ph):
                u, half = t + 2, HALVES[ph]
                act.wait_ge(wqk_mm, 2 * u + ph + 1)
                if u >= 1:
                    act.wait_ge(half_in[half], 96 * u)
                nc.scalar.activation(parts[:, 0, 512 * half:512 * half + 512], ps[:, prep_bank(u, "wqk", ph), :],
                                     ACT.Identity, bias=bqk[:, 0:1]).then_inc(qH_done, 1)

            def k_high(t, half):
                u = t + 2
                act.wait_ge(rope_done, rope_count(u, 1, half))
                if u >= 1:
                    act.wait_ge(half_in[half], 96 * u)
                nc.scalar.copy(parts[:, 2, 512 * half:512 * half + 512],
                               rope[:, 0, rope_at(u, 1, half)]).then_inc(kH_done, 1)

            def exps(t, c, pair):
                _, q, k, off, w = CHUNKS[c]
                act.wait_ge(score_mm, 2 * NC * t + 2 * c + pair + 1)
                if NC * t + c >= RING:
                    act.wait_ge(pv_mm, NC * t + c - RING + 1)
                nc.scalar.activation(probs[:, c % RING, 2 * pair:2 * pair + 2, 0:w], E[pair][:, :, 0:w],
                                     ACT.Exp).then_inc(exp_done, 1)

            def turned(v, ph):
                act.wait_ge(nm_tr, 2 * v + ph + 1)
                if v >= 1:
                    act.wait_ge(row_in[HALVES[ph]], 64 * v)
                nc.scalar.copy(nmT[HALVES[ph]], ps[0:8 * G, work(v - 1, "turn", ph), 0:128]).then_inc(nmT_done, 1)

            def o_copy(t, ph):
                q = HALVES[ph]
                act.wait_ge(pv_mm, NC * t + LAST[ph] + 1)
                if t >= 1:
                    act.wait_ge(o_tr, 2 * (t - 1) + ph + 1)
                nc.scalar.copy(oc[:, q], O).then_inc(o_done, 1)

            def late(kind, k):
                i = ORDER[k]
                b, s, n5 = i // 2, k % 2, slice(512 * i, 512 * i + 512)
                if kind == "yT":
                    act.wait_ge(yT_mm, k + 1)
                    if k >= 2:
                        act.wait_ge(x1_mm, k - 1)
                    nc.scalar.copy(yT[:, s, :], ps[:, LATE_BANK["yT"][k], :]).then_inc(yT_done, 1)
                elif kind == "z":
                    act.wait_ge(stats2, 4 * (k + 1))
                    nc.scalar.activation(std[:, 4 * i:4 * i + 4], mv[:, 4 * i:4 * i + 4, 1], ACT.Sqrt,
                                         bias=epsc[:, 0:1]).then_inc(std2, 1)
                elif kind == "zT":
                    act.wait_ge(zT_mm, k + 1)
                    act.wait_ge(score_mm, 2 * NC * (NU - 1))
                    nc.scalar.activation(h2T[:, n5], ps[:, LATE_BANK["zT"][k], :], ACT.Identity,
                                         bias=gate[:, SBC, b:b + 1], scale=gate[:, CB, b:b + 1]).then_inc(h2T_done, 1)
                elif kind == "router":
                    act.wait_ge(sc_mm, k + 1)
                    nc.scalar.copy(srow[:, n5], ps[:, LATE_BANK["router"][k], :]).then_inc(srow_done, 1)
                elif kind == "weights":
                    act.wait_ge(scol_done, k + 1)
                    nc.scalar.activation(sig[:, NT * k:NT * k + NT], scol[:, NT * k:NT * k + NT], ACT.Exp,
                                         scale=-1.0).then_inc(sig_done, 1)
                elif kind == "gelu":
                    for h in range(2):
                        act.wait_ge(half_in[h], 96 * NU)
                    for f in range(FT):
                        act.wait_ge(f1_mm, FT * k + f + 1)
                        if k >= 2:
                            act.wait_ge(f2_mm, k - 1)
                        nc.scalar.activation(actT[:, s, f, :], ps[:, F1_BANK[k][f], :], ACT.Gelu_apprx_tanh,
                                             bias=cols[:, B1 + f:B1 + f + 1]).then_inc(gelu_done, 1)

            def diagonals():
                act.wait_ge(gao_done, 1)
                for n, which in enumerate(ROWS):
                    for b in range(B):
                        ins = nc.scalar.activation(diag[:, n, b, :], ident, ACT.Copy, scale=gate[:, which, b:b + 1])
                ins.then_inc(diag_done, 1)

            def rows_out(n):
                act.wait_ge(bc_mm, n + 1)
                nc.scalar.copy(bc[:].rearrange("p r b c -> p (r b c)")[:, 512 * n:512 * n + 512],
                               ps[:, n, :]).then_inc(bc_done, 1)

            act.wait_ge(attn_in, 64)
            for kind, n in FIRST:
                if kind == "proj":
                    projected(-2, n)
                else:
                    q_high(-2, n)
                if (kind, n) in (("wqk", 0), ("proj", 7)):
                    k_high(-2, 1 if kind == "wqk" else 0)
            for t in range(-1, NU):
                for c in range(NC):
                    if t == -1 and c == MAPS_AT + 2:
                        diagonals()
                    if t == -1 and c - ROWS_AT in range(3):
                        rows_out(c - ROWS_AT)
                    for kind, n in STEPS[t][c]:
                        if kind == "scores" and t >= 0:
                            exps(t, c, n)
                            if n == 0 and c == COPY_STEP[0]:
                                o_copy(t, 0)
                            if n == 0 and c == COPY_STEP[1] and t >= 1:
                                o_copy(t - 1, 1)
                        elif kind == "proj" and t + 2 < NU:
                            projected(t, n)
                        elif kind == "wqk" and t + 2 < NU:
                            q_high(t, n)
                        elif kind == "turn" and 0 <= t + 1 < NU:
                            turned(t + 1, n)
                    if c in KH_STEP and t + 2 < NU:
                        k_high(t, KH_STEP[c])
                    for kind, k in LATE.get((t, c), ()):
                        late(kind, k)
            for kind, k in TAIL:
                if kind == "norm":
                    o_copy(NU - 1, 1)
                else:
                    late(kind, k)

        @block.gpsimd
        def _(pool):
            nc.gpsimd.memset(stack[0][SR:128].bitcast(F32), 0.0).then_inc(tails, 1)
            pool.wait_ge(tails, 1)
            nc.gpsimd.memset(stack[0][SR:SR + 2, 1].bitcast(F32), 1.0).then_inc(tails, 1)
            pool.wait_ge(tails, 2)

            def rotate(t, a, half):
                u = t + 2
                n, before_this = 512 * half, 4 * (u - 1) + 2 * a + HALVES.index(half)
                for rot, table in ((0, cosT), (1, sinT)):
                    pool.wait_ge(proj_ev, 8 * u + PROJ.index((a, half, rot)) + 1)
                    r = rope[:, rot, n:n + 512]
                    nc.gpsimd.tensor_tensor(r, r, table[:, n:n + 512], ALU.mult).then_inc(rope_step, 1)
                pool.wait_ge(rope_step, 2 * before_this + 2)
                nc.gpsimd.tensor_tensor(rope[:, 0, n:n + 512], rope[:, 0, n:n + 512], rope[:, 1, n:n + 512],
                                        ALU.add).then_inc(rope_done, 1)

            def k_low(t, half):
                u = t + 2
                pool.wait_ge(kH_done, 2 * u + HALVES.index(half) + 1)
                n = slice(512 * half, 512 * half + 512)
                nc.gpsimd.tensor_tensor(parts[:, 3, n], rope[:, 0, n], parts[:, 2, n].bitcast(F32),
                                        ALU.subtract).then_inc(kL_done, 1)

            def residual(k):
                i = ORDER[k]
                b = i // 2
                q = slice(4 * i, 4 * i + 4)
                pool.wait_ge(z2_done, k + 1)
                nc.gpsimd.tensor_tensor(res[:, q, :], z2[:, q, :], bc[:, 3, b:b + 1, :].to_broadcast([128, 4, C]),
                                        ALU.mult).then_inc(res_step, 1)
                pool.wait_ge(res_step, 2 * k + 1)
                nc.gpsimd.tensor_tensor(res[:, q, :], res[:, q, :], xs[:, q, :], ALU.add).then_inc(res_step, 1)
                pool.wait_ge(res_step, 2 * k + 2)
                nc.gpsimd.tensor_tensor(res[:, q, :], res[:, q, :], bc[:, 4, b:b + 1, :].to_broadcast([128, 4, C]),
                                        ALU.add).then_inc(res_done, 1)

            def constants(b):
                pool.wait_ge(bc_done, 3)
                pool.wait_ge(zn_done, QD)
                nc.gpsimd.tensor_tensor(xs[:, NT * b:NT * b + NT, :], xs[:, NT * b:NT * b + NT, :],
                                        bc[:, 1, b:b + 1, :].to_broadcast([128, NT, C]), ALU.add).then_inc(xadd_done, 1)
                pool.wait_ge(ffn_in, 32)
                nc.gpsimd.tensor_tensor(w2g[:, b], w2g[:, b], bc[:, 2, b:b + 1, :].to_broadcast([128, FT, C]),
                                        ALU.mult).then_inc(w2g_done, 1)

            pool.wait_ge(attn_in, 64)
            for t in range(-2, NU):
                for c in range(NC):
                    if t >= 0 and c in DIAG:
                        pool.wait_ge(exp_done, 2 * NC * t + 2 * c + 2)
                        p = probs[:, c % RING, :, 0:128]
                        nc.gpsimd.affine_select(out=p, in_=p, compare_op=ALU.is_ge, fill=0.0, base=0,
                                                pattern=[[0, G], [1, 128]], channel_multiplier=-1).then_inc(sel_done, 1)
                    if 1 <= t <= B and c == NC - 1:
                        constants(t - 1)
                    if -1 <= t and t + 2 < NU:
                        if c in ROPE_STEP:
                            rotate(t, *ROPE_STEP[c])
                        if c in KL_STEP:
                            k_low(t, KL_STEP[c])

            for k in range(2):
                residual(k)
            for kind, k in TAIL:
                if kind == "z":
                    residual(k)

        @block.vector
        def _(dve):
            chain = [0]

            def then(ins):
                chain[0] += 1
                ins.then_inc(dve_step, 1)
                dve.wait_ge(dve_step, chain[0])

            nc.vector.memset(epsc[:], EPS).then_inc(memsets, 1)
            nc.vector.memset(ones[:], 1.0).then_inc(memsets, 1)
            nc.vector.memset(onesb[:], 1.0).then_inc(memsets, 1)
            for p in range(2):
                nc.vector.memset(pm[p][:], NEG).then_inc(memsets, 1)
                then(nc.vector.memset(vu[p][:], 0.0))
                nc.vector.memset(vu[p][:, :, :, HD:HD + 1], 1.0).then_inc(memsets, 1)

            def norm_stats(i, done):
                for n in range(4 * i, 4 * i + 4):
                    ins = nc.vector.bn_stats(bst[:, n, :], xs[:, n, :])
                then(ins)
                for n in range(4 * i, 4 * i + 4):
                    nc.vector.bn_aggr(mv[:, n, :], bst[:, n, :]).then_inc(done, 1)

            def normalise(i, dst):
                then(nc.vector.reciprocal(rstd[:, 4 * i:4 * i + 4], std[:, 4 * i:4 * i + 4]))
                for n in range(4 * i, 4 * i + 4):
                    ins = nc.vector.tensor_scalar(dst[:, n, :], xs[:, n, :], mv[:, n, 0:1], rstd[:, n:n + 1],
                                                  ALU.subtract, ALU.mult)
                return ins

            def normalise_first(i):
                dve.wait_ge(std_done, i + 1)
                normalise(i, zn).then_inc(zn_done, 1)

            for i in range(2):
                dve.wait_ge(x_in[i], 16)
                norm_stats(i, stats)
            dve.wait_ge(silu_e, 1)
            then(nc.vector.tensor_scalar(sig[:, 2:4], sig[:, 0:2], 1.0, None, ALU.add))
            then(nc.vector.reciprocal(sig[:, 4:6], sig[:, 2:4]))
            nc.vector.tensor_tensor(sig[:, 6:8], sig[:, 4:6], cT, ALU.mult).then_inc(silu_done, 1)
            normalise_first(0)
            normalise_first(1)
            dve.wait_ge(mod_mm, 1)
            then(nc.vector.tensor_copy(modc[:].rearrange("p k b -> p (k b)"), ps[:, 6, 0:12]))
            nc.vector.tensor_scalar(gate[:, CA, :], modc[:, 1, :], 1.0, None, ALU.add).then_inc(gates_done, 1)
            nc.vector.tensor_copy(gate[:, SA, :], modc[:, 0, :]).then_inc(gates_done, 1)
            nc.vector.tensor_scalar(gate[:, CB, :], modc[:, 4, :], 1.0, None, ALU.add).then_inc(gates_done, 1)
            nc.vector.tensor_copy(gate[:, SBC, :], modc[:, 3, :]).then_inc(gates_done, 1)
            for i in range(2, QD):
                dve.wait_ge(x_in[i], 16)
                norm_stats(i, stats)
                normalise_first(i)

            def qk_low(i, a):
                dve.wait_ge(qkH_done, 2 * i + a + 1)
                n = slice(512 * i, 512 * i + 512)
                nc.vector.scalar_tensor_tensor(out=q8[:, 2 * a + 1, n], in0=ps[:, 2 + a, :],
                                               scalar=cols[:, BQ + a:BQ + a + 1], in1=q8[:, 2 * a, n].bitcast(F32),
                                               op0=ALU.add, op1=ALU.subtract).then_inc(qkL_done, 1)

            def v_copy(i):
                dve.wait_ge(v_mm, i + 1)
                nc.vector.tensor_tensor(vnat[:, 4 * i:4 * i + 4, :], ps[:, 4, :].rearrange("p (t c) -> p t c", c=C),
                                        bvb.rearrange("p (o c) -> p o c", o=1).to_broadcast([128, 4, C]),
                                        ALU.add).then_inc(v_done, 1)

            dve.wait_ge(const_in, 16)
            for i in range(QD):
                qk_low(i, 0)
                qk_low(i, 1)
                v_copy(i)
                if i == 1:
                    dve.wait_ge(attn_in, 64)
                    then(nc.vector.tensor_copy(whi, wraw))
                    nc.vector.tensor_copy(wsplit[0:64], wraw[0:64]).then_inc(wsplit_done, 1)
                    nc.vector.tensor_tensor(wsplit[64:SR], wraw[64:SR], whi[64:SR].bitcast(F32),
                                            ALU.subtract).then_inc(wsplit_done, 1)
                    nc.vector.tensor_scalar(wqk, wqk, float(L) ** -0.5, None, ALU.mult).then_inc(wsplit_done, 1)
                    nc.vector.tensor_scalar(bqk[:], cols[:, WB:WB + 1], float(L) ** -0.5, None,
                                            ALU.mult).then_inc(wsplit_done, 1)
            nc.vector.tensor_copy(identb[:], ident).then_inc(memsets, 1)
            nc.vector.tensor_scalar(maskb[:], tri, MASKED, None, ALU.mult).then_inc(memsets, 1)

            def gates():
                for src, dst in ((2, GA), (5, GB)):
                    g = modc[:, src, :]
                    then(nc.vector.tensor_scalar(sig[:, 8:10], g, 0.25, None, ALU.max))
                    then(nc.vector.scalar_tensor_tensor(out=sig[:, 10:12], in0=g, scalar=-1.0, in1=sig[:, 8:10],
                                                        op0=ALU.mult, op1=ALU.max))
                    then(nc.vector.tensor_scalar(sig[:, 12:14], g, 0.0, 2.0, ALU.is_ge, ALU.mult))
                    then(nc.vector.scalar_tensor_tensor(out=gate[:, dst, :], in0=sig[:, 12:14], scalar=-1.0,
                                                        in1=sig[:, 10:12], op0=ALU.add, op1=ALU.mult))
                then(nc.vector.tensor_tensor(gate[:, GBC, :], gate[:, GB, :], gate[:, CB, :], ALU.mult))
                then(nc.vector.tensor_tensor(gate[:, GBS, :], gate[:, GB, :], gate[:, SBC, :], ALU.mult))
                then(nc.vector.tensor_scalar(gate[:, GB2, :], gate[:, GB, :], cols[:, B2:B2 + 1], None, ALU.mult))

            def output_map():
                dve.wait_ge(m8_mm, 1)
                nc.vector.tensor_tensor(m8, ps[:, 6, 0:128], blockd, ALU.mult).then_inc(m8_done, 1)
                dve.wait_ge(yb_mm, 1)
                nc.vector.tensor_tensor(yb[:, 0:1], ps[:, 2, 0:1], cols[:, LOB:LOB + 1], ALU.add).then_inc(yb_done, 1)

            def output_constant():
                dve.wait_ge(yb_mm, 2)
                then(nc.vector.tensor_tensor(yb[:, 1:2], ps[:, 2, 1:2], cols[:, CPB:CPB + 1], ALU.add))
                nc.vector.tensor_scalar(gate[:, GAO, :], gate[:, GA, :], yb[:, 1:2], None,
                                        ALU.mult).then_inc(gao_done, 1)

            def output_map_gated():
                dve.wait_ge(wo_mm, 1)
                dve.wait_ge(bc_done, 3)
                for b in range(B):
                    ins = nc.vector.tensor_tensor(woT[:, b, :], ps[:, 6, 128:256], bc[:, 0, b, :], ALU.mult)
                ins.then_inc(wo_done, 1)

            def q_low(t, ph):
                u, half = t + 2, HALVES[ph]
                dve.wait_ge(qH_done, 2 * u + ph + 1)
                n = slice(512 * half, 512 * half + 512)
                nc.vector.scalar_tensor_tensor(out=parts[:, 1, n], in0=ps[:, prep_bank(u, "wqk", ph), :],
                                               scalar=bqk[:, 0:1], in1=parts[:, 0, n].bitcast(F32),
                                               op0=ALU.add, op1=ALU.subtract).then_inc(qL_done, 1)

            def row_max(t, m):
                _, i, part, j, heads = MAXES[m]
                v, w = t + 1, max_width(i, part)
                dve.wait_ge(max_mm, NM * v + m + 1)
                nc.vector.tensor_reduce(pm[v % 2][:, i // 4, i % 4, j:j + heads, part],
                                        ps[:, work(t, "max", m), 0:heads * w].rearrange("p (j n) -> p j n", n=w), AX.X,
                                        ALU.max).then_inc(max_done, 1)

            def row_minima(v, ph):
                half, n = HALVES[ph], 2 * v + ph
                dve.wait_ge(max_done, NM * v + NM_END[ph])
                if n >= 1:
                    dve.wait_ge(nm_tr, n)
                nc.vector.tensor_reduce(nm[:, half].rearrange("p j i -> p i j"), pm[v % 2][:, half], AX.X, ALU.max,
                                        negate=True).then_inc(nm_step, 1)
                dve.wait_ge(nm_step, 2 * n + 1)
                nc.vector.tensor_copy(nms[:, half, :, 0, :], nm[:, half]).then_inc(nm_step, 1)
                dve.wait_ge(nm_step, 2 * n + 2)
                nc.vector.tensor_tensor(nms[:, half, :, 1, :], nm[:, half], nms[:, half, :, 0, :].bitcast(F32),
                                        ALU.subtract).then_inc(nm_done, 1)

            def load_values(v):
                b, g = v // NG, v % NG
                if v >= 2:
                    dve.wait_ge(pv_mm, NC * (v - 1))
                nc.vector.tensor_copy(
                    vu[v % 2][:, :, :, 0:HD],
                    vnat[:, NT * b:NT * b + NT, G * HD * g:G * HD * (g + 1)].rearrange(
                        "p t (j e) -> p t j e", e=HD)).then_inc(vu_done, 1)

            def norm(t, ph):
                b, g, q = t // NG, t % NG, HALVES[ph]
                dve.wait_ge(o_tr, 2 * t + ph + 1)
                o = ps[:, work(min(t + ph, NU - 1), "norm", ph), :].rearrange("p (n c) -> p n c", c=32)
                rec = recd[:, ph, :].rearrange("p (n o) -> p n o", o=1)
                then(nc.vector.reciprocal(rec, o[:, :, HD:HD + 1]))
                t0 = NT * b + 4 * q
                nc.vector.tensor_tensor(
                    ynat[:, t0:t0 + 4, G * HD * g:G * HD * (g + 1)].rearrange("p t (j e) -> p t j e", e=HD),
                    o[:, :, 0:HD].rearrange("p (t j) e -> p t j e", j=G),
                    rec.rearrange("p (t j) o -> p t j o", j=G).to_broadcast([128, 4, G, HD]),
                    ALU.mult).then_inc(ynat_done, 1)

            def compare(b):
                S = srow[:, T * b:T * b + T]
                dve.wait_ge(scol_mm, b + 1)
                nc.vector.tensor_copy(scol[:, NT * b:NT * b + NT],
                                      ps[:, LATE_BANK["compare"][b], 0:NT]).then_inc(scol_done, 1)
                if b:
                    dve.wait_ge(rank_mm, b)
                else:
                    for done in (qH_done, qL_done, kH_done, kL_done, rope_done):
                        dve.wait_ge(done, 4 * NU if done is rope_done else 2 * NU)
                dve.wait_ge(scol_done, b + 1)
                if b:
                    dve.wait_ge(gt_done, COMPARES * b)
                for j in range(NT):
                    blk = slice(128 * j, 128 * (j + 1))
                    ins = nc.vector.scalar_tensor_tensor(out=eqm[:, blk], in0=S[:, blk],
                                                         scalar=scol[:, NT * b + j:NT * b + j + 1],
                                                         in1=tri, op0=ALU.is_equal, op1=ALU.mult)
                then(ins)
                for j in range(NT):
                    sj = scol[:, NT * b + j:NT * b + j + 1]
                    gj, blk = before[j], slice(128 * j, 128 * (j + 1))
                    if j:
                        nc.vector.tensor_scalar(gj[:, 0:128 * j], S[:, 0:128 * j], sj, None,
                                                ALU.is_lt).then_inc(gt_done, 1)
                    if j < NT - 1:
                        nc.vector.tensor_scalar(gj[:, 128 * (j + 1):], S[:, 128 * (j + 1):], sj, None,
                                                ALU.is_le).then_inc(gt_done, 1)
                    nc.vector.scalar_tensor_tensor(out=gj[:, blk], in0=S[:, blk], scalar=sj, in1=eqm[:, blk],
                                                   op0=ALU.is_lt, op1=ALU.add).then_inc(gt_done, 1)

            def late(kind, k):
                s = k % 2
                if kind == "compare":
                    compare(k)
                elif kind == "rank":
                    n = slice(NT * k, NT * k + NT)
                    dve.wait_ge(sig_done, k + 1)
                    then(nc.vector.tensor_scalar(sig[:, n], sig[:, n], 1.0, None, ALU.add))
                    then(nc.vector.reciprocal(sig[:, n], sig[:, n]))
                    dve.wait_ge(rank_mm, k + 1)
                    nc.vector.scalar_tensor_tensor(out=wsel[:, n], in0=ps[:, LATE_BANK["rank"][0], 0:NT],
                                                   scalar=float(KEEP), in1=sig[:, n], op0=ALU.is_lt,
                                                   op1=ALU.mult).then_inc(wsel_done, 1)
                elif kind == "x1":
                    i = ORDER[k]
                    dve.wait_ge(x1_mm, k + 1)
                    dve.wait_ge(xadd_done, B)
                    nc.vector.tensor_tensor(xs[:, 4 * i:4 * i + 4, :],
                                            ps[:, LATE_BANK["x1"][k], :].rearrange("p (t c) -> p t c", c=C),
                                            xs[:, 4 * i:4 * i + 4, :], ALU.add).then_inc(x1_done, 1)
                    dve.wait_ge(x1_done, k + 1)
                    norm_stats(i, stats2)
                elif kind == "z":
                    dve.wait_ge(std2, k + 1)
                    normalise(ORDER[k], z2).then_inc(z2_done, 1)
                elif kind == "f2":
                    i = ORDER[k]
                    dve.wait_ge(f2_mm, k + 1)
                    nc.vector.tensor_tensor(proc[:, 4 * i:4 * i + 4, :],
                                            ps[:, LATE_BANK["f2"][k], :].rearrange("p (t c) -> p t c", c=C),
                                            bc[:, 5, i // 2:i // 2 + 1, :].to_broadcast([128, 4, C]),
                                            ALU.add).then_inc(proc_done, 1)
                elif kind == "fin":
                    dve.wait_ge(wsel_done, k // 2 + 1)
                    dve.wait_ge(proc_done, k + 1)
                    dve.wait_ge(res_done, k + 1)
                    for t in range(4 * ORDER[k], 4 * ORDER[k] + 4):
                        nc.vector.scalar_tensor_tensor(out=fin[:, t, :], in0=proc[:, t, :], scalar=wsel[:, t:t + 1],
                                                       in1=res[:, t, :], op0=ALU.mult,
                                                       op1=ALU.add).then_inc(fin_done, 1)

            def rotate_first(a, half):
                n = 512 * half
                for rot, table in ((0, cosT), (1, sinT)):
                    dve.wait_ge(proj_ev, proj_count(0, PROJ.index((a, half, rot))))
                    r = rope[:, rot, rope_at(0, a, half)]
                    ins = nc.vector.tensor_tensor(r, r, table[:, n:n + 512], ALU.mult)
                then(ins)
                plain, rotated = (rope[:, rot, rope_at(0, a, half)] for rot in range(2))
                nc.vector.tensor_tensor(plain, plain, rotated, ALU.add).then_inc(rope_done, 1)

            def k_low_first(half):
                dve.wait_ge(kH_done, HALVES.index(half) + 1)
                n = slice(512 * half, 512 * half + 512)
                nc.vector.tensor_tensor(parts[:, 3, n], rope[:, 0, rope_at(0, 1, half)], parts[:, 2, n].bitcast(F32),
                                        ALU.subtract).then_inc(kL_done, 1)

            rotate_first(0, 1)
            rotate_first(1, 1)
            q_low(-2, 0)
            k_low_first(1)
            rotate_first(0, 0)
            q_low(-2, 1)
            rotate_first(1, 0)
            k_low_first(0)
            for t in range(-1, NU):
                v = t + 1
                for c in range(NC):
                    if t == -1 and c == MAPS_AT:
                        gates()
                        output_map()
                    if t == -1 and c == MAPS_AT + 1:
                        output_constant()
                    if t == -1 and c == ROWS_AT + 4:
                        output_map_gated()
                    if c == LAG + 1 and 0 <= v < NU:
                        load_values(v)
                    for kind, n in STEPS[t][c]:
                        if kind == "max" and 0 <= v < NU:
                            row_max(t, n)
                            if n + 1 in NM_END:
                                row_minima(v, NM_END.index(n + 1))
                        elif kind == "wqk" and t + 2 < NU:
                            q_low(t, n)
                        elif kind == "norm" and t - n >= 0:
                            norm(t - n, n)
                    for kind, k in LATE.get((t, c), ()):
                        late(kind, k)
            for kind, k in TAIL:
                if kind == "norm":
                    norm(NU - 1, 1)
                else:
                    late(kind, k)

        @block.tensor
        def _(pe):
            mm = nc.tensor.matmul

            def transposes(i):
                pe.wait_ge(zn_done, i + 1)
                if i >= 2:
                    pe.wait_ge(hT_done, i - 1)
                for n in range(4):
                    ins = nc.tensor.transpose(ps[:, i % 2, 128 * n:128 * n + 128], zn[:, 4 * i + n, :], ident)
                ins.then_inc(zn_tr, 1)

            pe.wait_ge(const_in, 16)
            transposes(0)
            pe.wait_ge(mod_in, 16)
            pe.wait_ge(silu_done, 1)
            for k in range(6):
                ins = mm(ps[:, 6, B * k:B * k + B], wmod[:, 128 * k:128 * k + 128], sig[:, 6:8], start=True, stop=True)
            ins.then_inc(mod_mm, 1)
            pe.wait_ge(qkv_in, 16)
            for i in range(QD):
                if i + 1 < QD:
                    transposes(i + 1)
                n5 = slice(512 * i, 512 * i + 512)
                pe.wait_ge(hT_done, i + 1)
                for a in range(2):
                    if i:
                        pe.wait_ge(qkL_done, 2 * i - 1 + a)
                    mm(ps[:, 2 + a, :], wqkvT[:, 128 * a:128 * a + 128], hT[:, n5], start=True,
                       stop=True).then_inc(qk_mm, 1)
                if i:
                    pe.wait_ge(v_done, i)
                for n in range(4):
                    ins = mm(ps[:, 4, 128 * n:128 * n + 128], hT[:, 512 * i + 128 * n:512 * i + 128 * n + 128],
                             wqkvT[:, 256:384], start=True, stop=True)
                ins.then_inc(v_mm, 1)

            def value_map():
                mm(ps[:, 6, 0:128], l2oT, kvrep, start=True, stop=True).then_inc(m8_mm, 1)
                mm(ps[:, 2, 0:1], l2oT, kvb, start=True, stop=True).then_inc(yb_mm, 1)

            def output_map():
                pe.wait_ge(yb_done, 1)
                mm(ps[:, 2, 1:2], cpT, yb[:, 0:1], start=True, stop=True).then_inc(yb_mm, 1)
                pe.wait_ge(m8_done, 1)
                mm(ps[:, 6, 128:256], m8, cpT, start=True, stop=True).then_inc(wo_mm, 1)

            def rows(n):
                pe.wait_ge(diag_done, 1)
                mm(ps[:, n, :], ones[:], diag.rearrange("p r b c -> p (r b c)")[:, 512 * n:512 * n + 512], start=True,
                   stop=True).then_inc(bc_mm, 1)

            last = {}

            def bank_free(kind, n, u, t=None, bank=None):
                bank = work(t, kind, n) if bank is None else bank
                content_read(bank)
                last[bank] = (kind, n, u)
                return ps[:, bank, :]

            def content_read(bank):
                if bank in last:
                    before_kind, m, v = last[bank]
                    if before_kind == "proj":
                        pe.wait_ge(proj_ev, proj_count(v, m))
                    elif before_kind == "wqk":
                        pe.wait_ge(qH_done, 2 * v + m + 1)
                        pe.wait_ge(qL_done, 2 * v + m + 1)
                    elif before_kind == "turn":
                        pe.wait_ge(nmT_done, 2 * v + m + 1)
                    elif before_kind == "norm":
                        pe.wait_ge(ynat_done, 2 * v + m + 1)
                    elif before_kind == "yT":
                        pe.wait_ge(yT_done, m + 1)
                    elif before_kind == "x1":
                        pe.wait_ge(x1_done, m + 1)
                    elif before_kind == "zT":
                        pe.wait_ge(h2T_done, m + 1)
                    elif before_kind == "router":
                        pe.wait_ge(srow_done, m + 1)
                    elif before_kind == "compare":
                        pe.wait_ge(scol_done, m + 1)
                    elif before_kind == "rank":
                        pe.wait_ge(wsel_done, m + 1)
                    elif before_kind == "f1":
                        pe.wait_ge(gelu_done, FT * m + v + 1)
                    elif before_kind == "f2":
                        pe.wait_ge(proc_done, m + 1)
                    else:
                        pe.wait_ge(max_done, NM * v + m + 1)

            def project(t, n):
                a, half, rot = PROJ[n]
                u = t + 2
                if n == 0:
                    pe.wait_ge(s8_in, 48 * (u + 1))
                mm(bank_free("proj", n, u, bank=prep_bank(u, "proj", n)), wsplit[:, 2 * a + rot, :],
                   s8[:, a, 512 * half:512 * half + 512], start=True, stop=True).then_inc(proj_mm, 1)

            def map_q(t, ph):
                u, half = t + 2, HALVES[ph]
                pe.wait_ge(rope_done, rope_count(u, 0, half))
                mm(bank_free("wqk", ph, u, bank=prep_bank(u, "wqk", ph)), wqk, rope[:, 0, rope_at(u, 0, half)],
                   start=True, stop=True).then_inc(wqk_mm, 1)

            def max_scores(t, m):
                ph, i, part, j0, heads = MAXES[m]
                v, w = t + 1, max_width(i, part)
                st = stack[v % 2]
                k0 = 512 * part
                diagonal = k0 + w == 128 * (i + 1)
                if m == 0:
                    pe.wait_ge(half_in[1], 96 * (v + 1))
                if part == 0:
                    pe.wait_ge(half_in[0], 96 * (v + 1))
                bank = bank_free("max", m, v, t)[:, 0:heads * w].rearrange("p (j n) -> p j n", n=w)
                for j in range(heads):
                    ins = mm(bank[:, j, :], st[0:SR, 0, j0 + j, 128 * i:128 * i + 128], st[0:SR, 1, j0 + j, k0:k0 + w],
                             start=True, stop=not diagonal, skip_group_check=True)
                if diagonal:
                    ins = mm(bank[:, :, w - 128:w], identb[:],
                             maskb[:].rearrange("p (o n) -> p o n", o=1).to_broadcast([128, heads, 128]),
                             start=False, stop=True, skip_group_check=True)
                ins.then_inc(max_mm, 1)

            def turn(v, ph):
                pe.wait_ge(nm_done, 2 * v + ph + 1)
                bank = bank_free("turn", ph, v, v - 1)
                nc.tensor.transpose(bank[0:8 * G, 0:128],
                                    nms[:, HALVES[ph]].bitcast(F32).rearrange("p j s i -> p (j s i)"),
                                    ident).then_inc(nm_tr, 1)

            def scores(t, c, pair):
                _, q, k, off, w = CHUNKS[c]
                st = stack[t % 2]
                if NC * t + c >= 1:
                    pe.wait_ge(exp_done, 2 * NC * t + 2 * (c - 1) + pair + 1)
                for n in range(2):
                    j = 2 * pair + n
                    ins = mm(E[pair][:, n, 0:w], st[:, 1, j, 128 * k:128 * k + 128],
                             st[:, 0, j, 512 * q + off:512 * q + 512], start=True, stop=True)
                ins.then_inc(score_mm, 1)

            def values(t, c):
                ph, q, k, off, w = CHUNKS[c]
                if c in DIAG:
                    pe.wait_ge(sel_done, len(DIAG) * t + DIAG.index(c) + 1)
                else:
                    pe.wait_ge(exp_done, 2 * NC * t + 2 * c + 2)
                if k == 0 and 2 * t + ph > 0:
                    pe.wait_ge(o_done, 2 * t + ph)
                for j in range(G):
                    ins = mm(O[32 * j:32 * j + 32, off:512], vu[t % 2][:, k, j, :], probs[:, c % RING, j, 0:w],
                             start=(k == 0), stop=(c in LAST), skip_group_check=True)
                ins.then_inc(pv_mm, 1)

            def norm(t, ph):
                pe.wait_ge(o_done, 2 * t + ph + 1)
                bank = bank_free("norm", ph, t, min(t + ph, NU - 1))
                for n in range(4):
                    ins = nc.tensor.transpose(bank[:, 128 * n:128 * n + 128],
                                              oc[:, HALVES[ph], 128 * n:128 * n + 128], ident)
                ins.then_inc(o_tr, 1)

            def late(kind, k):
                i = ORDER[k]
                b, s, n5 = i // 2, k % 2, slice(512 * i, 512 * i + 512)
                if kind in LATE_BANK:
                    bank = bank_free(kind, k, 0, bank=LATE_BANK[kind][k])
                if kind == "yT":
                    pe.wait_ge(ynat_done, 2 * (NG * b + NG - 1) + HALVES.index(i % 2) + 1)
                    for n in range(4):
                        ins = nc.tensor.transpose(bank[:, 128 * n:128 * n + 128], ynat[:, 4 * i + n, :], ident)
                    ins.then_inc(yT_mm, 1)
                elif kind == "x1":
                    pe.wait_ge(yT_done, k + 1)
                    for n in range(4):
                        ins = mm(bank[:, 128 * n:128 * n + 128], yT[:, s, 128 * n:128 * n + 128], woT[:, b, :],
                                 start=True, stop=True)
                    ins.then_inc(x1_mm, 1)
                elif kind == "zT":
                    pe.wait_ge(z2_done, k + 1)
                    for n in range(4):
                        ins = nc.tensor.transpose(bank[:, 128 * n:128 * n + 128], z2[:, 4 * i + n, :], ident)
                    ins.then_inc(zT_mm, 1)
                elif kind == "router":
                    pe.wait_ge(h2T_done, k + 1)
                    pe.wait_ge(ffn_in, 32)
                    mm(bank, wrb, h2T[:, n5], start=True, stop=True).then_inc(sc_mm, 1)
                elif kind == "compare":
                    pe.wait_ge(srow_done, 2 * (k + 1))
                    for n in range(NT):
                        ins = nc.tensor.transpose(bank[:, n:n + 1], srow[0:1, T * k + 128 * n:T * k + 128 * n + 128],
                                                  ident[0:1, 0:1])
                    ins.then_inc(scol_mm, 1)
                elif kind == "f1":
                    if k >= 2:
                        pe.wait_ge(exp_done, 2 * NC * NU)
                    for f in range(FT):
                        mm(bank_free("f1", k, f, bank=F1_BANK[k][f]), w1[:, 128 * f:128 * f + 128], h2T[:, n5],
                           start=True, stop=True).then_inc(f1_mm, 1)
                elif kind == "f2":
                    pe.wait_ge(gelu_done, FT * (k + 1))
                    pe.wait_ge(w2g_done, B)
                    if k >= 2:
                        pe.wait_ge(o_done, 2 * NU)
                    for n in range(4):
                        for f in range(FT):
                            ins = mm(bank[:, 128 * n:128 * n + 128], actT[:, s, f, 128 * n:128 * n + 128],
                                     w2g[:, b, f, :], start=(f == 0), stop=(f == FT - 1))
                    ins.then_inc(f2_mm, 1)
                elif kind == "rank":
                    pe.wait_ge(gt_done, COMPARES * (k + 1))
                    for n in range(NT):
                        for j in range(NT):
                            ins = mm(bank[:, n:n + 1], before[j][:, 128 * n:128 * n + 128], onesb[:, 0:1],
                                     start=(j == 0), stop=(j == NT - 1))
                    ins.then_inc(rank_mm, 1)

            pe.wait_ge(wsplit_done, 4)
            for kind, n in FIRST:
                if (kind, n) == ("proj", 2):
                    pe.wait_ge(qkL_done, 2 * QD)
                if (kind, n) == ("wqk", 1):
                    pe.wait_ge(v_done, QD)
                (project if kind == "proj" else map_q)(-2, n)
            pe.wait_ge(proj_ev, 8)
            for t in range(-1, NU):
                for c in range(NC):
                    if t == -1 and c == MAPS_AT:
                        value_map()
                    if t == -1 and c == MAPS_AT + 1:
                        output_map()
                    if t == -1 and c - ROWS_AT in range(3):
                        rows(c - ROWS_AT)
                    if t == 0 and c == 0:
                        pe.wait_ge(bc_done, 3)
                        content_read(3)
                        pe.wait_ge(wo_done, 1)
                    if c in (0, LAST[0] + 1) and t >= 0:
                        pe.wait_ge(row_in[HALVES[CHUNKS[c][0]]], 64 * (t + 1))
                    if c == 0 and t >= 0:
                        pe.wait_ge(tails_in, 16)
                        pe.wait_ge(vu_done, t + 1)
                    for kind, n in STEPS[t][c]:
                        if kind == "scores" and t >= 0:
                            scores(t, c, n)
                        elif kind == "values" and c >= LAG and t >= 0:
                            values(t, c - LAG)
                        elif kind == "values" and c < LAG and t >= 1:
                            values(t - 1, NC + c - LAG)
                        elif kind == "max" and 0 <= t + 1 < NU:
                            if t == -1 and n == 0:
                                pe.wait_ge(memsets, 9)
                            max_scores(t, n)
                        elif kind == "proj" and t + 2 < NU:
                            project(t, n)
                        elif kind == "wqk" and t + 2 < NU:
                            map_q(t, n)
                        elif kind == "turn" and 0 <= t + 1 < NU:
                            turn(t + 1, n)
                        elif kind == "norm" and t - n >= 0:
                            norm(t - n, n)
                    for kind, k in LATE.get((t, c), ()):
                        late(kind, k)
            for c in range(NC - LAG, NC):
                values(NU - 1, c)
            for kind, k in TAIL:
                if kind == "norm":
                    norm(NU - 1, 1)
                else:
                    late(kind, k)


def lay_out(i):
    f = {k: np.asarray(v) for k, v in i.items()}
    cols = np.zeros((128, 16), np.float32)
    wc, bcn = f["L0_attn_c_attn_w"], f["L0_attn_c_attn_b"]
    swap = np.arange(L) ^ 1
    cols[:, 0], cols[:, 1] = bcn[0:C], bcn[C:2 * C]
    cols[:, 2] = np.repeat(f["L0_attn_q2l_b"], G)
    cols[:, 3] = np.repeat(f["L0_attn_q2l_b"][swap], G)
    cols[:, 4] = np.repeat(f["L0_attn_kv2l_b"], G)
    cols[:, 5] = np.repeat(f["L0_attn_kv2l_b"][swap], G)
    cols[:, 6] = np.repeat(f["L0_attn_wqk_b"], G)
    cols[:, 7] = np.tile(f["L0_attn_l2o_b"], H)
    cols[:, 8] = f["L0_attn_cproj_b"]
    cols[:, 9] = f["L0_ffn_b2"]
    cols[:, 10:10 + FT] = f["L0_ffn_b1"].reshape(FT, 128).T
    wlat = np.zeros((3, G, HD, 4, L, G), np.float32)
    wqk = np.zeros((L, G, L, G), np.float32)
    for j in range(G):
        for k, w in enumerate((f["L0_attn_q2l_w"], f["L0_attn_q2l_w"][swap],
                               f["L0_attn_kv2l_w"], f["L0_attn_kv2l_w"][swap])):
            wlat[:, j, :, k, :, j] = w.T
        wqk[:, j, :, j] = f["L0_attn_wqk_w"].T
    inv = (np.float32(1.0) / np.float32(10000.0) ** (np.arange(0, L, 2, dtype=np.float32) / np.float32(L)))
    ang = np.repeat(np.outer(np.arange(T, dtype=np.float32), inv.astype(np.float32)), 2, axis=1).astype(np.float32)
    sign = np.where(np.arange(L) % 2 == 0, -1.0, 1.0)
    cos = np.repeat(np.cos(ang.astype(np.float64)).T, G, axis=0).astype(np.float32)
    sin = np.repeat((np.sin(ang.astype(np.float64)) * sign).T, G, axis=0).astype(np.float32)
    at = np.arange(128)
    tri = (at[None, :] > at[:, None]).astype(np.float32)
    blockd = (at[None, :] // HD == at[:, None] // HD).astype(np.float32)
    return {
        "x": f["L0_attn_x"],
        "consts": np.concatenate([np.eye(128, dtype=np.float32), np.broadcast_to(bcn[2 * C:], (128, C)), cols], 1),
        "tables": np.concatenate([cos, sin], 1),
        "mod": np.concatenate([f["L0_c"].T, f["L0_wmod"]], 1),
        "qkv": np.concatenate([wc.T, blockd], 1),
        "wlat": wlat.reshape(SR, 4, 128),
        "weights": np.concatenate([wqk.reshape(128, 128), f["L0_attn_cproj_w"].T, tri,
                                   np.broadcast_to(f["L0_ffn_w_router"][:, None], (C, 128)), f["L0_ffn_W1"]], 1),
        "vmap": np.concatenate([np.tile(f["L0_attn_l2o_w"].T, (1, H)), np.tile(f["L0_attn_kv2l_w"], (1, H)),
                                f["L0_attn_kv2l_b"].reshape(L, 1)], 1),
        "w2": f["L0_ffn_W2"].reshape(FT, 128, C).transpose(1, 0, 2),
    }


def kernel(**inputs):
    import concourse.bacc as bacc
    from concourse.bass_utils import run_bass_kernel_spmd

    nc = bacc.Bacc("TRN2", target_bir_lowering=False, num_devices=1)
    arrays, d = {}, {}
    for name, a in lay_out(inputs).items():
        a = np.ascontiguousarray(a)
        arrays[f"in_{name}"] = a
        d[name] = nc.dram_tensor(f"in_{name}", a.shape, mybir.dt.from_np(a.dtype), kind="ExternalInput").ap()
    out = nc.dram_tensor("out_x", (B, T, C), F32, kind="ExternalOutput").ap()
    adaln_block(nc, d, out)
    r = run_bass_kernel_spmd(nc, [arrays], core_ids=[0])
    return r.results[0]["out_x"]
```
